# Optimizing a Trainium2 kernel written in Bass

```python
import numpy as np
import jax
import jax.numpy as jnp

def _softmax(x, axis=-1):
    return jax.nn.softmax(x, axis=axis)

def _gelu(x):
    return jax.nn.gelu(x, approximate=True)

def _silu(x):
    return jax.nn.silu(x)

def _sigmoid(x):
    return jax.nn.sigmoid(x)

def _layernorm(x, axis=-1, eps=1e-05):
    m = jnp.mean(x, axis=axis, keepdims=True)
    v = jnp.var(x, axis=axis, keepdims=True)
    return (x - m) / jnp.sqrt(v + eps)

def _scatter_add(tgt, idx, src, axis=0):
    return tgt.at[idx].add(src)

def _segment_sum(src, seg, n):
    return jax.ops.segment_sum(src, seg, n)
kernel_name = 'mk_decoder_preln_d1_seqx_r8_0be98c'

def setup_inputs(seed: int=0):
    np.random.seed(seed)
    _w = jnp.asarray

    def _rec_inputs():
        import jax
        import jax.numpy as jnp
        _rk = jax.random.key(seed)
        x = -0.0003929 + 0.9999 * jax.random.normal(jax.random.fold_in(_rk, 1), (4, 512, 128), jnp.float32)
        _lenS = 512 - jax.random.randint(jax.random.fold_in(_rk, 7), (4,), 0, max(1, 512 // 4) + 1, jnp.int32)
        _lenS2 = 77 - jax.random.randint(jax.random.fold_in(_rk, 8), (4,), 0, max(1, 77 // 4) + 1, jnp.int32)
        _ctx_768P = jax.random.normal(jax.random.fold_in(_rk, 11), (4, 16, 96), jnp.float32)
        _ctx_768c = jax.random.dirichlet(jax.random.fold_in(_rk, 511), 0.3 * jnp.ones((16,), jnp.float32), (4, 77))
        _ctx_768t = jnp.einsum('bsk,bkd->bsd', _ctx_768c, _ctx_768P)
        _ctx_768t = _ctx_768t * jax.lax.rsqrt(jnp.mean(jnp.square(_ctx_768t)) + 1e-12) * 0.953939
        ctx_768 = 2.09791e-05 + 1.00001 * (_ctx_768t + 0.3 * jax.random.normal(jax.random.fold_in(_rk, 611), (4, 77, 96), jnp.float32))
        return (x, ctx_768)
    x, ctx_768 = _rec_inputs()

    def _L0_attn_setup():
        import jax, jax.numpy as jnp
        import numpy as np
        B, L, D = (2, 256, 128)
        H, HD = (16, 64)
        LD = 32
        key = jax.random.key(seed)
        ks = jax.random.split(key, 6)
        s = lambda fan_in: 1.0 / np.sqrt(fan_in)
        x_bld = jax.random.normal(ks[0], (B, L, D), dtype=jnp.float32)
        Wq = jax.random.normal(ks[1], (D, H, HD), dtype=jnp.float32) * s(D)
        Wkv_down = jax.random.normal(ks[2], (D, LD), dtype=jnp.float32) * s(D)
        Wk_up = jax.random.normal(ks[3], (LD, H, HD), dtype=jnp.float32) * s(LD)
        Wv_up = jax.random.normal(ks[4], (LD, H, HD), dtype=jnp.float32) * s(LD)
        Wout = jax.random.normal(ks[5], (H, HD, D), dtype=jnp.float32) * s(H * HD)
        return {'x_bld': x_bld, 'Wq': Wq, 'Wkv_down': Wkv_down, 'Wk_up': Wk_up, 'Wv_up': Wv_up, 'Wout': Wout}
    _L0_attn_all = _L0_attn_setup()
    _L0_attn_in = {k: v for k, v in _L0_attn_all.items() if k in ('Wq', 'Wkv_down', 'Wk_up', 'Wv_up', 'Wout')}
    del _L0_attn_all

    def _L0_xattn_setup():
        import jax, jax.numpy as jnp
        import numpy as np
        HEADS = 8
        DIM_HEAD = 64
        QUERY_DIM = 128
        CONTEXT_DIM = 96
        INNER = HEADS * DIM_HEAD
        key = jax.random.key(seed)
        ks = jax.random.split(key, 7)
        B, Sq, Skv = (4, 512, 128)
        x = jax.random.normal(ks[0], (B, Sq, QUERY_DIM), dtype=jnp.float32)
        context = jax.random.normal(ks[1], (B, Skv, CONTEXT_DIM), dtype=jnp.float32)
        Wq = jax.random.normal(ks[2], (QUERY_DIM, INNER), dtype=jnp.float32) * QUERY_DIM ** (-0.5)
        Wk = jax.random.normal(ks[3], (CONTEXT_DIM, INNER), dtype=jnp.float32) * CONTEXT_DIM ** (-0.5)
        Wv = jax.random.normal(ks[4], (CONTEXT_DIM, INNER), dtype=jnp.float32) * CONTEXT_DIM ** (-0.5)
        Wo = jax.random.normal(ks[5], (INNER, QUERY_DIM), dtype=jnp.float32) * INNER ** (-0.5)
        bo = jax.random.normal(ks[6], (QUERY_DIM,), dtype=jnp.float32) * 0.01
        return {'x': x, 'context': context, 'Wq': Wq, 'Wk': Wk, 'Wv': Wv, 'Wo': Wo, 'bo': bo}
    _L0_xattn_all = _L0_xattn_setup()
    _L0_xattn_in = {k: v for k, v in _L0_xattn_all.items() if k in ('Wq', 'Wk', 'Wv', 'Wo', 'bo')}
    del _L0_xattn_all

    def _L0_ffn_setup():
        import jax, jax.numpy as jnp
        import numpy as np
        B, T, D, H, E, TOPK = (2, 256, 128, 512, 8, 2)

        def sq_relu(x):
            return jnp.square(jax.nn.relu(x))
        key = jax.random.key(seed)
        ks = jax.random.split(key, 6)
        s = 0.02
        return {'x': jax.random.normal(ks[0], (B, T, D), dtype=jnp.float32), 'W_router': jax.random.normal(ks[1], (D, E), dtype=jnp.float32) * s, 'W_up': jax.random.normal(ks[2], (E, D, H), dtype=jnp.float32) * s, 'W_down': jax.random.normal(ks[3], (E, H, D), dtype=jnp.float32) * s, 'W_sh_up': jax.random.normal(ks[4], (D, H), dtype=jnp.float32) * s, 'W_sh_down': jax.random.normal(ks[5], (H, D), dtype=jnp.float32) * s}
    _L0_ffn_all = _L0_ffn_setup()
    _L0_ffn_in = {k: v for k, v in _L0_ffn_all.items() if k in ('W_router', 'W_up', 'W_down', 'W_sh_up', 'W_sh_down')}
    del _L0_ffn_all
    return {'x': x, 'ctx_768': ctx_768, 'L0_attn_Wq': _L0_attn_in['Wq'], 'L0_attn_Wkv_down': _L0_attn_in['Wkv_down'], 'L0_attn_Wk_up': _L0_attn_in['Wk_up'], 'L0_attn_Wv_up': _L0_attn_in['Wv_up'], 'L0_attn_Wout': _L0_attn_in['Wout'], 'L0_xattn_Wq': _L0_xattn_in['Wq'], 'L0_xattn_Wk': _L0_xattn_in['Wk'], 'L0_xattn_Wv': _L0_xattn_in['Wv'], 'L0_xattn_Wo': _L0_xattn_in['Wo'], 'L0_xattn_bo': _L0_xattn_in['bo'], 'L0_ffn_W_router': _L0_ffn_in['W_router'], 'L0_ffn_W_up': _L0_ffn_in['W_up'], 'L0_ffn_W_down': _L0_ffn_in['W_down'], 'L0_ffn_W_sh_up': _L0_ffn_in['W_sh_up'], 'L0_ffn_W_sh_down': _L0_ffn_in['W_sh_down']}

def reference(x, ctx_768, L0_attn_Wq, L0_attn_Wkv_down, L0_attn_Wk_up, L0_attn_Wv_up, L0_attn_Wout, L0_xattn_Wq, L0_xattn_Wk, L0_xattn_Wv, L0_xattn_Wo, L0_xattn_bo, L0_ffn_W_router, L0_ffn_W_up, L0_ffn_W_down, L0_ffn_W_sh_up, L0_ffn_W_sh_down):
    import jax
    import jax.numpy as jnp

    def _L0_attn_ref(x_bld, Wq, Wkv_down, Wk_up, Wv_up, Wout):
        import jax, jax.numpy as jnp
        import numpy as np
        B, L, D = (2, 256, 128)
        H, HD = (16, 64)
        LD = 32
        q_blhd = jnp.einsum('bld,dhk->blhk', x_bld, Wq)
        latent_bll = jnp.einsum('bld,dc->blc', x_bld, Wkv_down)
        k_blhd = jnp.einsum('blc,chk->blhk', latent_bll, Wk_up)
        v_blhd = jnp.einsum('blc,chk->blhk', latent_bll, Wv_up)
        attn = jnp.einsum('bqhd,bkhd->bhqk', q_blhd, k_blhd) / jnp.sqrt(jnp.asarray(HD, dtype=x_bld.dtype))
        l = x_bld.shape[1]
        mask = (jnp.arange(l)[None, :] <= jnp.arange(l)[:, None])[None, None]
        neg_inf = jnp.finfo(attn.dtype).min
        attn = jax.nn.softmax(jnp.where(mask, attn, neg_inf), axis=-1)
        y_blhd = jnp.einsum('bhqk,bkhd->bqhd', attn, v_blhd)
        return jnp.einsum('bqhd,hdo->bqo', y_blhd, Wout)

    def _L0_xattn_ref(x, context, Wq, Wk, Wv, Wo, bo):
        import jax, jax.numpy as jnp
        import numpy as np
        HEADS = 8
        DIM_HEAD = 64
        QUERY_DIM = 128
        CONTEXT_DIM = 96
        INNER = HEADS * DIM_HEAD
        B, Sq, _ = x.shape
        h, d = (HEADS, DIM_HEAD)
        scale = d ** (-0.5)
        q = (x @ Wq).reshape(B, Sq, h, d).transpose(0, 2, 1, 3)
        k = (context @ Wk).reshape(B, -1, h, d).transpose(0, 2, 1, 3)
        v = (context @ Wv).reshape(B, -1, h, d).transpose(0, 2, 1, 3)
        scores = jnp.einsum('bhid,bhjd->bhij', q, k) * scale
        attn = jax.nn.softmax(scores, axis=-1)
        out = jnp.einsum('bhij,bhjd->bhid', attn, v)
        out = out.transpose(0, 2, 1, 3).reshape(B, Sq, h * d)
        return out @ Wo + bo

    def _L0_ffn_ref(x, W_router, W_up, W_down, W_sh_up, W_sh_down):
        import jax, jax.numpy as jnp
        import numpy as np
        B, T, D, H, E, TOPK = (2, 256, 128, 512, 8, 2)

        def sq_relu(x):
            return jnp.square(jax.nn.relu(x))
        Bb, Tt, Dd = x.shape
        x_flat = x.reshape(-1, Dd)
        N = x_flat.shape[0]
        logits = x_flat @ W_router
        probs = jax.nn.sigmoid(logits)
        topk_probs, topk_idx = jax.lax.top_k(probs, TOPK)
        topk_probs = topk_probs / (jnp.sum(topk_probs, axis=-1, keepdims=True) + 1e-06)
        combine = jnp.zeros((N, E), dtype=x.dtype).at[jnp.arange(N)[:, None], topk_idx].add(topk_probs)
        out = sq_relu(x_flat @ W_sh_up) @ W_sh_down
        for e in range(E):
            h = sq_relu(x_flat @ W_up[e])
            out = out + combine[:, e:e + 1] * (h @ W_down[e])
        return out.reshape(Bb, Tt, Dd)
    x = x + _L0_attn_ref(_layernorm(x, axis=-1), L0_attn_Wq, L0_attn_Wkv_down, L0_attn_Wk_up, L0_attn_Wv_up, L0_attn_Wout)
    x = x + _L0_xattn_ref(_layernorm(x, axis=-1), ctx_768, L0_xattn_Wq, L0_xattn_Wk, L0_xattn_Wv, L0_xattn_Wo, L0_xattn_bo)
    x = x + _L0_ffn_ref(_layernorm(x, axis=-1), L0_ffn_W_router, L0_ffn_W_up, L0_ffn_W_down, L0_ffn_W_sh_up, L0_ffn_W_sh_down)
    return x

_drawn_inputs = setup_inputs


def setup_inputs(seed=0):
    import zlib

    import numpy as np

    out = dict(_drawn_inputs(seed))
    spreads = {}
    factors = {'L0_xattn_bo': 6.135,
     'L0_ffn_W_router': 3.832,
     'L0_ffn_W_up': 3.635,
     'L0_ffn_W_down': 3.296,
     'L0_ffn_W_sh_up': 3.176,
     'L0_ffn_W_sh_down': 2.827}
    for name, (base, spread) in spreads.items():
        noise = np.random.default_rng([zlib.crc32(name.encode()), seed]).standard_normal(out[name].shape)
        drawn = base * np.exp(spread * noise) if base else spread * noise
        out[name] = jnp.asarray(drawn.astype(out[name].dtype))
    for name, factor in factors.items():
        out[name] = (out[name] * factor).astype(out[name].dtype)
    return out
```

```python
from contextlib import ExitStack

import concourse.bass as bass
from concourse import mybir

F32 = mybir.dt.float32
F32R = mybir.dt.float32r
BF16 = mybir.dt.bfloat16
ALU = mybir.AluOpType
ACT = mybir.ActivationFunctionType
AX = mybir.AxisListType

P = 128
EPS = 1e-5
NEG = -1e30


def decoder_layer(nc, x, ctxT, wqT, wkT, wvT, wout, wkv, cwqT, cwk, cwv, cwo, cbo, wr, wup, wdown, vscr, out):
    B, L, D = x.shape
    NT = B * L // P
    TB = L // P
    LD = wkv.shape[1]
    HD = 64
    H = wqT.shape[1] * 2
    HG = P // LD
    G = H // HG
    NU = B * G
    CD, SK = ctxT.shape[0], ctxT.shape[2]
    CH = cwqT.shape[1] * 2
    KV = CH * SK
    KC = -(-KV // P)
    KL = KV - (KC - 1) * P
    E = wr.shape[1]
    NE = E + 1
    HC = wup.shape[2] // P
    R3 = 3 * LD
    RM = R3 + 2

    with ExitStack() as ctx:
        def sb(name, shape, dt=F32):
            return ctx.enter_context(nc.sbuf_tensor(name, shape, dt))

        def sem(name):
            return ctx.enter_context(nc.semaphore(name))

        xs = sb("xs", [P, NT, D])
        xn = sb("xn", [P, NT, D])
        xnT = sb("xnT", [P, NT * P])
        ident = sb("ident", [P, P])
        identb = sb("identb", [P, P], BF16)
        mask_qk = sb("mask_qk", [P, P], BF16)
        mask_kq = sb("mask_kq", [P, P], BF16)
        w_qT = sb("w_qT", [P, H // 2, D])
        w_kT = sb("w_kT", [P, H // 2, LD])
        w_vT = sb("w_vT", [P, H // 2, LD])
        w_out = sb("w_out", [P, H // 2, D])
        w_kv3 = sb("w_kv3", [P, R3])
        wA = sb("wA", [P, H * LD])
        wB = sb("wB", [P, G, D])
        c_qT = sb("c_qT", [P, CH // 2, D])
        c_k = sb("c_k", [CD, CH * HD])
        c_v = sb("c_v", [CD, CH * HD])
        c_o = sb("c_o", [P, CH // 2, D])
        c_T = sb("c_T", [CD, B * SK])
        c_bo = sb("c_bo", [P, D])
        c_kT = sb("c_kT", [P, CH // 2, B * SK])
        c_vT = sb("c_vT", [P, CH // 2, B * SK])
        c_G = sb("c_G", [P, B, KV])
        c_V1 = sb("c_V1", [SK, 2, 4, D])
        c_V = sb("c_V", [P, B, KC, D])
        w_r = sb("w_r", [P, E])
        stats = sb("stats", [P, NT, 6])
        mv = sb("mv", [P, NT, 2])
        rstd = sb("rstd", [P, NT])
        big = sb("big", [P, 2 * H * L])
        qstack = [big[0:RM, i * H * L:(i + 1) * H * L].rearrange("p (h t) -> p h t", h=H).bitcast(F32R)
                  for i in range(2)]
        lstack = sb("lstack", [RM, NT * P], F32R)
        laug = sb("laug", [P, NT, 2 * LD])
        qhi = sb("qhi", [P, G, L], F32R)
        qlo = sb("qlo", [P, G, L], F32R)
        negm = sb("negm", [P, 2, TB, HG])
        mparts = sb("mparts", [P, 2, TB, 2 * HG], F32R)
        mT = sb("mT", [2 * HG, 2, L], F32R)
        probT = sb("probT", [P, 4, 2, L])
        ypair = sb("ypair", [P, 2, L])
        rden = sb("rden", [P, TB, 2])
        yn = sb("yn", [P, 2, TB, P])
        ynT = xn[:, :, :].rearrange("p (g j) d -> p g (j d)", g=G)

        ps = ctx.enter_context(nc.psum_tensor("ps", [P, 8, 512], F32))

        s = {}
        for name in ("x_in w_in cw_in f_in consts lnstat lnroot rootdone xn_ready t_full t_free xnT_ready "
                     "setup_full setup_free vout0 vout1 vback ones_ready "
                     "scores maxed mparts_ready mT_ready mrow0 mrow1 st exped pv ydrained ynormed ynT_ready "
                     "misc_full misc_free qhi_ready qlo_ready lhi_ready llo_ready laug_ready qstack0 qstack1 attn_done "
                     "dchain achain pchain fw0 fw1 "
                     "x2n x2nT_full x2nT_free cscores csub cexp pn_ready cpt_full cpt_free cout_full cout_free "
                     "cpsum_free f_xn xT_full xT_free lg_full lg_exp lg_done up_full relu_done sq_dve sq_pool down_full acc_done y_out").split():
            s[name] = sem("s_" + name)
        block = ctx.enter_context(nc.Block())

        SIT = [(0, (0, 1, 2, 3)), (1, (0, 1)), (1, (2, 3))] + [(j, (h,)) for j in (2, 3) for h in range(HG)]
        NS = len(SIT)
        PER = [2, 2, 2, 1, 1, 1, 1, 1]
        FROM = [sum(PER[:i]) for i in range(8)]
        NI = 8

        def slot_misc(u, t):
            b, g = divmod(u, G)
            uses = []
            if t == 1 and u >= 1:
                uses.append(("yt", 2 * u - 1))
            if t == 2 and u >= 1:
                uses.append(("back", u - 1))
            if t == 3 and g == 0 and u >= 1:
                uses.append(("out", b - 1))
            if t == 6:
                uses.append(("yt", 2 * u))
            if b + 1 < B:
                for at, use in (((0, 0), ("latT", b + 1)), ((0, 4), ("q", (b + 1, 0))), ((0, 5), ("q", (b + 1, 1))),
                                ((0, 7), ("q", (b + 1, 2))), ((1, 0), ("q", (b + 1, 3))), ((1, 3), ("lat", b + 1))):
                    if at == (g, t):
                        uses.append(use)
            if t == 7 and u + 2 < NU:
                uses.append(("m", u + 2))
            return uses

        PRO = [("latT", 0)] + [("q", (0, g)) for g in range(G)] + [("lat", 0)]
        EPI = [("yt", 2 * NU - 1), ("back", NU - 1), ("out", B - 1)]
        order = PRO + [("m", 0), ("m", 1)]
        for u in range(NU):
            for t in range(8):
                order += slot_misc(u, t)
        order += EPI
        MISC = {use: i for i, use in enumerate(order)}
        MB = 7
        YB = 6
        UPN = NE * HC * B

        wait_for = {"x": 16, "w": 16 * 5, "cw": 16 * 6, "f": 16 * 3}

        f_up = w_qT[:, :, :].rearrange("p (i c) n -> p i (c n)", i=2)
        f_dn = w_out[:, :, :].rearrange("p (i c) n -> p i c n", i=2)
        hr = qhi[:, :, :].bitcast(F32)
        probf = probT[:, :, :, :].rearrange("p a b n -> p (a b n)")
        hs = probf.rearrange("p (i c n) -> p i c n", i=2, c=HC)
        acc = xs

        sx = probf[:, 0:2 * KV].rearrange("p (i n) -> p i n", i=2)
        pr = probf[:, 2 * KV:4 * KV].rearrange("p (i n) -> p i n", i=2)
        pT = qhi[:, :, :].bitcast(F32).rearrange("p g n -> p (g n)")[:, 0:2 * KC * P].rearrange("p (i c n) -> p i c n", i=2, c=KC)
        cstat = sb("cstat", [P, 2, 3, CH])
        sg = sb("sg", [P, 3, NT, E])
        ranks = [v.rearrange("p (t e j) -> p t e j", t=NT, e=E) for v in
                 (ypair[:, :, :].rearrange("p i n -> p (i n)"), yn[:, :, :, :].rearrange("p i j n -> p (i j n)"))]
        ltm = sb("ltm", [P, E, E])
        ssum = sb("ssum", [P, 2, NT])

        setup = [("xT", i) for i in range(B)] + [("A", 0), ("A", 1), ("B", 0), ("B", 1)] \
            + [("kT", i) for i in range(CH // 2)] + [("vT", i) for i in range(CH // 2)] + [("G", h) for h in range(CH)] \
            + [("V", i) for i in range(2 * B)]
        SET = {k: i for i, k in enumerate(setup)}
        vset0 = SET[("V", 0)]
        SB = 6

        @block.sync
        def _(sp):
            for b in range(B):
                sp.dma_start(xs[:, b * TB:(b + 1) * TB, :], x[b, :, :].rearrange("(j p) d -> p j d", p=P)
                             ).then_inc(s["x_in"], 16)
            for dst, src in ((w_qT, wqT), (w_kT, wkT), (w_vT, wvT), (w_out, wout)):
                sp.dma_start(dst[:, :, :], src).then_inc(s["w_in"], 16)
            sp.dma_start(w_kv3[:, 0:LD], wkv).then_inc(s["w_in"], 16)
            for dst, src in ((c_k, cwk), (c_v, cwv)):
                sp.dma_start(dst[:, :], src).then_inc(s["cw_in"], 16)
            for dst, src in ((c_qT, cwqT), (c_o, cwo)):
                sp.dma_start(dst[:, :, :], src).then_inc(s["cw_in"], 16)
            sp.dma_start(c_T[:, :], ctxT.rearrange("c b s -> c (b s)")).then_inc(s["cw_in"], 16)
            sp.dma_start(c_bo[:, :], cbo).then_inc(s["cw_in"], 16)

            def stack(b):
                q = qstack[b % 2]
                if b >= 2:
                    sp.wait_ge(s["st"], NI * G * (b - 1))
                for row, part, ready, count in ((0, qhi, "qhi_ready", G * (b + 1)), (LD, qhi, "qhi_ready", G * (b + 1)),
                                                (2 * LD, qlo, "misc_free", MISC[("q", (b, G - 1))] + 1)):
                    sp.wait_ge(s[ready], count)
                    for i in range(HG):
                        dst = q[row:row + LD, :, :].rearrange("p (g i) t -> p g i t", i=HG)[:, :, i, :]
                        sp.dma_start(dst.bitcast(F32), part[i * LD:(i + 1) * LD, :, :].bitcast(F32)).then_inc(s[f"qstack{b % 2}"], 16)

            def mrows(u):
                b, g = divmod(u, G)
                sp.wait_ge(s["misc_free"], MISC[("m", u)] + 1)
                for r in range(2):
                    sp.dma_start(qstack[b % 2][R3 + r:R3 + r + 1, g * HG:(g + 1) * HG, :].bitcast(F32),
                                 mT[r * HG:(r + 1) * HG, u % 2, :].bitcast(F32)).then_inc(s[f"mrow{u % 2}"], 16)

            stack(0)
            mrows(0)
            mrows(1)
            for u in range(NU - 2):
                b, g = divmod(u, G)
                if g == 1 and b + 1 < B:
                    stack(b + 1)
                mrows(u + 2)

            outv = out.rearrange("b (j p) d -> p b j d", p=P)

            def store(b):
                sp.wait_ge(s["acc_done"], NE * TB * (b + 1))
                sp.dma_start(outv[:, b, :, :], acc[:, b * TB:(b + 1) * TB, :]).then_inc(s["y_out"], 16)

            sp.wait_ge(s["st"], NI * NU)
            sp.dma_start(w_r[:, :], wr).then_inc(s["f_in"], 16)
            for k in range(B * NE):
                if k >= 2:
                    sp.wait_ge(s["down_full"], k - 1)
                sp.dma_start(f_up[:, k % 2, :], wup[:, k % NE, :]).then_inc(s[f"fw{k % 2}"], 16)
                sp.dma_start(f_dn[:, k % 2, :, :], wdown[:, k % NE, :, :]).then_inc(s[f"fw{k % 2}"], 16)
                if k % NE == 2 and k > NE:
                    store(k // NE - 1)
            store(B - 1)

            sp.wait_ge(s["y_out"], 16 * B)

        @block.gpsimd
        def _(pool):
            n = [0]

            def chain(ins):
                n[0] += 1
                ins.then_inc(s["pchain"], 1)
                pool.wait_ge(s["pchain"], n[0])

            chain(nc.gpsimd.memset(laug[:, :, LD:2 * LD], 1.0))
            chain(nc.gpsimd.memset(lstack[R3:RM, :].bitcast(F32), 1.0))
            chain(nc.gpsimd.memset(ident[:, :], 0.0))
            nc.gpsimd.affine_select(out=ident[:, :], in_=ident[:, :], compare_op=ALU.not_equal, fill=1.0, base=0,
                                    pattern=[[-1, P]], channel_multiplier=1).then_inc(s["consts"], 1)
            pool.wait_ge(s["consts"], 1)
            chain(nc.gpsimd.memset(identb[:, :], 0.0))
            nc.gpsimd.affine_select(out=identb[:, :], in_=identb[:, :], compare_op=ALU.not_equal, fill=1.0, base=0,
                                    pattern=[[-1, P]], channel_multiplier=1).then_inc(s["consts"], 1)
            pool.wait_ge(s["consts"], 2)
            chain(nc.gpsimd.memset(mask_qk[:, :], 0.0))
            nc.gpsimd.affine_select(out=mask_qk[:, :], in_=mask_qk[:, :], compare_op=ALU.is_ge, fill=NEG, base=0,
                                    pattern=[[-1, P]], channel_multiplier=1).then_inc(s["consts"], 1)
            pool.wait_ge(s["consts"], 3)
            chain(nc.gpsimd.memset(mask_kq[:, :], 0.0))
            nc.gpsimd.affine_select(out=mask_kq[:, :], in_=mask_kq[:, :], compare_op=ALU.is_ge, fill=NEG, base=0,
                                    pattern=[[1, P]], channel_multiplier=-1).then_inc(s["consts"], 1)
            pool.wait_ge(s["consts"], 4)
            chain(nc.gpsimd.memset(ltm[:, :, :], 1.0))
            nc.gpsimd.affine_select(out=ltm[:, :, :], in_=ltm[:, :, :], compare_op=ALU.is_gt, fill=0.0, base=0,
                                    pattern=[[1, E], [-1, E]], channel_multiplier=0).then_inc(s["consts"], 1)

            for i in range(2 * B):
                b, half = divmod(i, 2)
                pool.wait_ge(s["setup_free"], vset0 + i + 1)
                pool.dma_start(vscr[b, half:CH:2, :, :].rearrange("h s d -> s h d"),
                             c_V1[:, i % 2, :, :]).then_inc(s[f"vout{i % 2}"], 16)
                if i % 2 == 1:
                    pool.wait_ge(s["vout0"], 16 * (b + 1))
                    pool.wait_ge(s["vout1"], 16 * (b + 1))
                    flat = vscr[b, :, :, :].rearrange("h s d -> (h s) d")
                    pool.dma_start(c_V[:, b, 0:KC - 1, :], flat[0:(KC - 1) * P, :].rearrange("(c p) d -> p c d", p=P)
                                 ).then_inc(s["vback"], 16)
                    pool.dma_start(c_V[0:KL, b, KC - 1, :], flat[(KC - 1) * P:KV, :]).then_inc(s["vback"], 16)

            pool.wait_ge(s["consts"], 5)
            for n2 in range(0, UPN, 2):
                e_i, c = divmod(n2, HC)
                pool.wait_ge(s["relu_done"], n2 + 1)
                if n2:
                    pool.wait_ge(s["sq_pool"], n2 // 2)
                if e_i >= 2:
                    pool.wait_ge(s["down_full"], e_i - 1)
                nc.gpsimd.tensor_tensor(hs[:, e_i % 2, c, :], hr[:, n2 % 4, :], hr[:, n2 % 4, :], ALU.mult
                                        ).then_inc(s["sq_pool"], 1)

        @block.scalar
        def _(act):
            def root(k):
                act.wait_ge(s["lnstat"], k + 1)
                nc.scalar.activation(rstd[:, :], rstd[:, :], ACT.Sqrt).then_inc(s["lnroot"], 1)

            root(0)
            for k in setup:
                i = SET[k]
                kind, a = k
                act.wait_ge(s["setup_full"], i + 1)
                pb = ps[:, i % SB, :]
                if kind == "xT":
                    ins = nc.scalar.activation(xnT[:, a * L:(a + 1) * L], pb, ACT.Copy)
                elif kind == "A":
                    ins = nc.scalar.activation(
                        wA[:, :].rearrange("p (h two c) -> p h two c", two=2, c=LD)[:, :, a, :],
                        pb[:, 0:H // 2 * LD].rearrange("p (h c) -> p h c", c=LD), ACT.Copy, scale=float(HD) ** -0.5)
                elif kind == "B":
                    for q in (a * LD, (a + 2) * LD):
                        ins = nc.scalar.activation(wB[q:q + LD, :, :], pb[q:q + LD, :].rearrange(
                            "p (g n) -> p g n", g=G), ACT.Copy)
                elif kind == "kT":
                    ins = nc.scalar.activation(c_kT[:, a, :], pb[:, 0:B * SK], ACT.Copy)
                elif kind == "vT":
                    ins = nc.scalar.activation(c_vT[:, a, :], pb[:, 0:B * SK], ACT.Copy)
                elif kind == "G":
                    ins = nc.scalar.activation(
                        c_G[:, :, a * SK:(a + 1) * SK], pb[:, 0:B * SK].rearrange("p (b s) -> p b s", b=B), ACT.Copy,
                        scale=float(HD) ** -0.5)
                else:
                    if a >= 2:
                        act.wait_ge(s[f"vout{a % 2}"], 16 * (a // 2))
                    ins = nc.scalar.activation(c_V1[:, a % 2, :, :], pb[0:SK, :].rearrange("p (h n) -> p h n", h=4),
                                               ACT.Copy)
                ins.then_inc(s["setup_free"], 1)

            def misc(use):
                i = MISC[use]
                kind, a = use
                pb = ps[:, MB, :]
                if kind == "q":
                    b, g = a
                    act.wait_ge(s["misc_full"], i + 1)
                    if b >= 1 and g == 0:
                        act.wait_ge(s[f"qstack{(b - 1) % 2}"], 16 * 3 * HG * ((b - 1) // 2 + 1))
                    nc.scalar.activation(qhi[:, g, :], pb, ACT.Copy).then_inc(s["qhi_ready"], 1)
                elif kind == "latT":
                    act.wait_ge(s["misc_full"], i + 1)
                    nc.scalar.activation(lstack[0:R3, a * L:(a + 1) * L], pb[0:R3, :], ACT.Copy
                                         ).then_inc(s["lhi_ready"], 1)
                elif kind == "m":
                    act.wait_ge(s["misc_full"], i + 1)
                    if a >= 2:
                        act.wait_ge(s[f"mrow{a % 2}"], 32 * (a // 2))
                    nc.scalar.activation(mT[:, a % 2, :], pb[0:2 * HG, :], ACT.Copy).then_inc(s["misc_free"], 1)
                elif kind == "back":
                    act.wait_ge(s["misc_full"], i + 1)
                    b, g = divmod(a, G)
                    if g == 0 and b >= 1:
                        act.wait_ge(s["misc_full"], MISC[("out", b - 1)] + 1)
                    nc.scalar.activation(ynT[:, g, :], pb, ACT.Copy).then_inc(s["misc_free"], 1)

            def yev(r):
                act.wait_ge(s["pv"], 4 * (r + 1))
                if r >= 2:
                    act.wait_ge(s["misc_full"], MISC[("yt", r - 2)] + 1)
                nc.scalar.activation(ypair[:, r % 2, :], ps[:, YB, :], ACT.Copy).then_inc(s["ydrained"], 1)

            for use in PRO:
                misc(use)
            misc(("m", 0))
            misc(("m", 1))
            for u in range(NU):
                for t in range(8):
                    n = NI * u + t
                    pair, i = divmod(t, TB)
                    w = L - i * P
                    act.wait_ge(s["st"], n + 1)
                    if n >= 4:
                        act.wait_ge(s["pv"], n - 3)
                    nc.scalar.activation(probT[:, n % 4, :, 0:w], ps[:, 2 + 2 * (n % 2):4 + 2 * (n % 2), 0:w], ACT.Exp
                                         ).then_inc(s["exped"], 1)
                    if t == 0 and u >= 1:
                        yev(2 * u - 1)
                    if t == 4:
                        yev(2 * u)
                    for use in slot_misc(u, t):
                        misc(use)
            yev(2 * NU - 1)
            misc(EPI[1])

            root(1)
            for t in range(NT + 4):
                if t < NT:
                    act.wait_ge(s["x2nT_full"], t + 1)
                    if t >= 2:
                        act.wait_ge(s["cscores"], t - 1)
                    nc.scalar.activation(xnT[:, t * P:(t + 1) * P], ps[:, 0, 0:P], ACT.Copy).then_inc(s["x2nT_free"], 1)
                k = t - 2
                if 0 <= k < NT:
                    act.wait_ge(s["csub"], k + 1)
                    if k >= 2:
                        act.wait_ge(s["pn_ready"], k - 1)
                    nc.scalar.activation(pr[:, k % 2, :], sx[:, k % 2, :], ACT.Exp).then_inc(s["cexp"], 1)
                k = t - 3
                if 0 <= k < NT:
                    act.wait_ge(s["cpt_full"], k + 1)
                    if k >= 2:
                        act.wait_ge(s["cout_full"], k - 1)
                    nc.scalar.activation(pT[:, k % 2, 0:4, :], ps[:, 5, :].rearrange("p (c n) -> p c n", c=4), ACT.Copy
                                         ).then_inc(s["cpt_free"], 1)
                    nc.scalar.activation(pT[0:KL, k % 2, 4, :], ps[0:KL, 6, 0:P], ACT.Copy).then_inc(s["cpt_free"], 1)

            root(2)
            for b in range(B):
                act.wait_ge(s["xT_full"], b + 1)
                nc.scalar.activation(xnT[:, b * L:(b + 1) * L], ps[:, b % 2, :], ACT.Copy).then_inc(s["xT_free"], 1)
            act.wait_ge(s["lg_full"], 1)
            nc.scalar.activation(sg[:, 0, :, :], ps[:, 2, 0:NT * E].rearrange("p (t e) -> p t e", e=E), ACT.Exp,
                                 scale=-1.0).then_inc(s["lg_exp"], 1)
            for n in range(UPN):
                act.wait_ge(s["up_full"], n + 1)
                if n >= 4:
                    act.wait_ge(s["sq_pool" if n % 2 == 0 else "sq_dve"], (n - 4) // 2 + 1)
                nc.scalar.activation(hr[:, n % 4, :], ps[:, 3 + n % 3, :], ACT.Relu).then_inc(s["relu_done"], 1)

        @block.vector
        def _(dve):
            n = [0]

            def chain(ins):
                n[0] += 1
                ins.then_inc(s["dchain"], 1)
                dve.wait_ge(s["dchain"], n[0])

            def norm_stats(k):
                for t in range(NT):
                    if t < NT - 1:
                        nc.vector.bn_stats(stats[:, t, :], xs[:, t, :])
                    else:
                        chain(nc.vector.bn_stats(stats[:, t, :], xs[:, t, :]))
                for t in range(NT):
                    if t < NT - 1:
                        nc.vector.bn_aggr(mv[:, t, :], stats[:, t, :])
                    else:
                        chain(nc.vector.bn_aggr(mv[:, t, :], stats[:, t, :]))
                nc.vector.tensor_scalar_add(rstd[:, :], mv[:, :, 1], EPS).then_inc(s["lnstat"], 1)
                dve.wait_ge(s["lnroot"], k + 1)
                chain(nc.vector.reciprocal(rstd[:, :], rstd[:, :]))

            def norm(t):
                return nc.vector.tensor_scalar(xn[:, t, :], xs[:, t, :], mv[:, t, 0:1], rstd[:, t:t + 1],
                                               ALU.subtract, ALU.mult)

            dve.wait_ge(s["w_in"], 80)
            for r in (1, 2):
                chain(nc.vector.tensor_copy(w_kv3[:, r * LD:(r + 1) * LD], w_kv3[:, 0:LD]))
            dve.wait_ge(s["x_in"], 16 * B)
            norm_stats(0)
            for t in range(NT):
                norm(t).then_inc(s["xn_ready"], 1)

            def maxes(u, k):
                j, heads = SIT[k]
                nn = NS * u + k
                dve.wait_ge(s["scores"], nn + 1)
                if u >= 2 and k == 0:
                    dve.wait_ge(s["mparts_ready"], u - 1)
                w = (j + 1) * P
                nh = len(heads)
                nc.vector.tensor_reduce(negm[:, u % 2, j, heads[0]:heads[0] + nh],
                                        ps[:, nn % 2, 0:nh * w].rearrange("p (h n) -> p h n", h=nh), AX.X, ALU.max,
                                        negate=True).then_inc(s["maxed"], 1)

            def split_max(u):
                dve.wait_ge(s["maxed"], NS * (u + 1))
                if u >= 2:
                    dve.wait_ge(s["misc_full"], MISC[("m", u - 2)] + 1)
                chain(nc.vector.tensor_copy(mparts[:, u % 2, :, 0:HG], negm[:, u % 2, :, :]))
                nc.vector.tensor_tensor(mparts[:, u % 2, :, HG:2 * HG], negm[:, u % 2, :, :],
                                        mparts[:, u % 2, :, 0:HG].bitcast(F32), ALU.subtract
                                        ).then_inc(s["mparts_ready"], 1)

            def misc(use):
                i = MISC[use]
                kind, a = use
                pb = ps[:, MB, :]
                if kind == "q":
                    b, g = a
                    dve.wait_ge(s["qhi_ready"], G * b + g + 1)
                    nc.vector.tensor_tensor(qlo[:, g, :], pb, qhi[:, g, :].bitcast(F32), ALU.subtract
                                            ).then_inc(s["misc_free"], 1)
                elif kind == "latT":
                    dve.wait_ge(s["lhi_ready"], a + 1)
                    nc.vector.tensor_tensor(lstack[LD:2 * LD, a * L:(a + 1) * L], pb[LD:2 * LD, :],
                                            lstack[LD:2 * LD, a * L:(a + 1) * L].bitcast(F32), ALU.subtract
                                            ).then_inc(s["misc_free"], 1)
                elif kind == "lat":
                    dve.wait_ge(s["misc_full"], i + 1)
                    nc.vector.tensor_copy(laug[:, a * TB:(a + 1) * TB, 0:LD],
                                          pb[:, 0:TB * LD].rearrange("p (j c) -> p j c", j=TB)
                                          ).then_inc(s["misc_free"], 1)
                elif kind == "yt":
                    dve.wait_ge(s["misc_full"], i + 1)
                    v = pb.rearrange("p (j h c) -> p j h c", j=TB, h=2)
                    chain(nc.vector.reciprocal(rden[:, :, :], v[:, :, :, LD]))
                    u, half = divmod(a, 2)
                    if u >= 2 and half == 0:
                        dve.wait_ge(s["misc_full"], MISC[("back", u - 2)] + 1)
                    nc.vector.tensor_tensor(
                        yn[:, u % 2, :, half * 2 * LD:(half + 1) * 2 * LD].rearrange("p j (h c) -> p j h c", h=2),
                        v[:, :, :, 0:LD], rden[:, :, :].unsqueeze(3).broadcast_to([P, TB, 2, LD]), ALU.mult
                    ).then_inc(s["misc_free"], 1)
                elif kind == "out":
                    dve.wait_ge(s["misc_full"], i + 1)
                    nc.vector.tensor_tensor(xs[:, a * TB:(a + 1) * TB, :], pb.rearrange("p (j n) -> p j n", j=TB),
                                            xs[:, a * TB:(a + 1) * TB, :], ALU.add).then_inc(s["misc_free"], 1)

            for use in PRO:
                misc(use)
            for u in (0, 1):
                for k in range(NS):
                    maxes(u, k)
                split_max(u)
            for u in range(NU):
                for t in range(8):
                    if u + 2 < NU:
                        for k in range(FROM[t], FROM[t] + PER[t]):
                            maxes(u + 2, k)
                        if t == 7:
                            split_max(u + 2)
                    for use in slot_misc(u, t):
                        misc(use)
            misc(EPI[0])
            misc(EPI[2])
            dve.wait_ge(s["misc_free"], len(order))

            norm_stats(1)
            dve.wait_ge(s["cw_in"], 96)
            for t in range(NT + 4):
                if t < NT:
                    norm(t).then_inc(s["x2n"], 1)
                k = t - 1
                if 0 <= k < NT:
                    dve.wait_ge(s["cscores"], k + 1)
                    sc = ps[:, 1 + 2 * (k % 2):3 + 2 * (k % 2), 0:KV // 2].rearrange("p a (h s) -> p a h s", s=SK)
                    mx = cstat[:, k % 2, 0, :].rearrange("p (a h) -> p a h", a=2)
                    chain(nc.vector.tensor_reduce(mx, sc, AX.X, ALU.max))
                    if k >= 2:
                        dve.wait_ge(s["cexp"], k - 1)
                    nc.vector.tensor_tensor(
                        sx[:, k % 2, :].rearrange("p (a h s) -> p a h s", a=2, s=SK), sc,
                        mx.unsqueeze(3).broadcast_to([P, 2, CH // 2, SK]), ALU.subtract).then_inc(s["csub"], 1)
                k = t - 2
                if 0 <= k < NT:
                    dve.wait_ge(s["cexp"], k + 1)
                    pv = pr[:, k % 2, :].rearrange("p (h s) -> p h s", s=SK)
                    chain(nc.vector.tensor_reduce(cstat[:, k % 2, 1, :], pv, AX.X, ALU.add))
                    chain(nc.vector.reciprocal(cstat[:, k % 2, 2, :], cstat[:, k % 2, 1, :]))
                    nc.vector.tensor_tensor(pv, pv, cstat[:, k % 2, 2, :].unsqueeze(2).broadcast_to([P, CH, SK]),
                                            ALU.mult).then_inc(s["pn_ready"], 1)
                k = t - 4
                if 0 <= k < NT:
                    chain(nc.vector.tensor_tensor(xs[:, k, :], xs[:, k, :], c_bo[:, :], ALU.add))
                    dve.wait_ge(s["cout_full"], k + 1)
                    nc.vector.tensor_tensor(xs[:, k, :], ps[:, 7, 0:P], xs[:, k, :], ALU.add
                                            ).then_inc(s["cout_free"], 1)
            dve.wait_ge(s["cout_free"], NT)

            norm_stats(2)
            for t in range(NT):
                norm(t).then_inc(s["f_xn"], 1)
            dve.wait_ge(s["lg_exp"], 1)
            chain(nc.vector.tensor_scalar_add(sg[:, 1, :, :], sg[:, 0, :, :], 1.0))
            chain(nc.vector.reciprocal(sg[:, 0, :, :], sg[:, 1, :, :]))
            pj = sg[:, 0, :, :].unsqueeze(2).broadcast_to([P, NT, E, E])
            pe_ = sg[:, 0, :, :].unsqueeze(3).broadcast_to([P, NT, E, E])
            dve.wait_ge(s["consts"], 5)
            chain(nc.vector.tensor_tensor(ranks[0], pj, pe_, ALU.is_equal))
            chain(nc.vector.tensor_tensor(ranks[0], ranks[0],
                                          ltm[:, :, :].unsqueeze(1).broadcast_to([P, NT, E, E]), ALU.mult))
            chain(nc.vector.tensor_tensor(ranks[1], pj, pe_, ALU.is_gt))
            chain(nc.vector.tensor_tensor(ranks[0], ranks[0], ranks[1], ALU.add))
            chain(nc.vector.tensor_reduce(sg[:, 1, :, :], ranks[0], AX.X, ALU.add))
            chain(nc.vector.tensor_single_scalar(sg[:, 1, :, :], sg[:, 1, :, :], 1.5, ALU.is_lt))
            chain(nc.vector.tensor_tensor(sg[:, 2, :, :], sg[:, 1, :, :], sg[:, 0, :, :], ALU.mult))
            chain(nc.vector.tensor_reduce(ssum[:, 0, :], sg[:, 2, :, :], AX.X, ALU.add))
            chain(nc.vector.tensor_scalar_add(ssum[:, 0, :], ssum[:, 0, :], 1e-6))
            chain(nc.vector.reciprocal(ssum[:, 1, :], ssum[:, 0, :]))
            chain(nc.vector.tensor_tensor(sg[:, 0, :, :], sg[:, 2, :, :],
                                          ssum[:, 1, :].unsqueeze(2).broadcast_to([P, NT, E]), ALU.mult))

            def accumulate(k):
                b, e = divmod(k, NE)
                dve.wait_ge(s["down_full"], k + 1)
                if k >= 1:
                    dve.wait_ge(s["acc_done"], TB * k)
                for j in range(TB):
                    t = b * TB + j
                    wt = 1.0 if e == NE - 1 else sg[:, 0, t, e:e + 1]
                    nc.vector.scalar_tensor_tensor(acc[:, t, :], ps[:, 6 + k % 2, j * P:(j + 1) * P], wt,
                                                   acc[:, t, :], ALU.mult, ALU.add).then_inc(s["acc_done"], 1)

            for n2 in range(1, UPN, 2):
                k, c = divmod(n2, HC)
                dve.wait_ge(s["relu_done"], n2 + 1)
                if k >= 2:
                    dve.wait_ge(s["down_full"], k - 1)
                nc.vector.tensor_tensor(hs[:, k % 2, c, :], hr[:, n2 % 4, :], hr[:, n2 % 4, :], ALU.mult
                                        ).then_inc(s["sq_dve"], 1)
                if c == HC - 1 and k >= 1:
                    accumulate(k - 1)
            accumulate(B * NE - 1)

        @block.tensor
        def _(pe):
            pe.wait_ge(s["consts"], 1)
            for k in setup:
                i = SET[k]
                kind, a = k
                if i >= SB:
                    pe.wait_ge(s["setup_free"], i - SB + 1)
                bank = i % SB
                if kind == "xT":
                    pe.wait_ge(s["xn_ready"], TB * (a + 1))
                    for j in range(TB):
                        last = nc.tensor.transpose(ps[:, bank, j * P:(j + 1) * P], xn[:, a * TB + j, :], ident[:, :])
                elif kind == "A":
                    pe.wait_ge(s["w_in"], 80)
                    r = a * HD
                    for i in range(H // 2):
                        last = nc.tensor.matmul(ps[:, bank, i * LD:(i + 1) * LD], w_qT[r:r + HD, i, :],
                                                w_kT[r:r + HD, i, :], start=True, stop=True)
                elif kind == "B":
                    r = a * HD
                    for h in range(a, H, 2):
                        q = (h % HG) * LD
                        last = nc.tensor.matmul(ps[q:q + LD, bank, (h // HG) * D:(h // HG + 1) * D],
                                                w_vT[r:r + HD, h // 2, :], w_out[r:r + HD, h // 2, :],
                                                start=True, stop=True)
                elif kind in ("kT", "vT"):
                    pe.wait_ge(s["cw_in"], 96)
                    w = c_k if kind == "kT" else c_v
                    last = nc.tensor.matmul(ps[:, bank, 0:B * SK], w[:, a * P:(a + 1) * P], c_T[:, :],
                                            start=True, stop=True)
                elif kind == "G":
                    r = (a % 2) * HD
                    pe.wait_ge(s["setup_free"], SET[("kT", a // 2)] + 1)
                    last = nc.tensor.matmul(ps[:, bank, 0:B * SK], c_qT[r:r + HD, a // 2, :], c_kT[r:r + HD, a // 2, :],
                                            start=True, stop=True)
                else:
                    b, half = divmod(a, 2)
                    pe.wait_ge(s["setup_free"], SET[("vT", CH // 2 - 1)] + 1)
                    r = half * HD
                    for hh in range(4):
                        h = 2 * hh + half
                        last = nc.tensor.matmul(ps[0:SK, bank, hh * D:(hh + 1) * D],
                                                c_vT[r:r + HD, h // 2, b * SK:(b + 1) * SK],
                                                c_o[r:r + HD, h // 2, :], start=True, stop=True)
                last.then_inc(s["setup_full"], 1)
            pe.wait_ge(s["setup_free"], len(setup))
            pe.wait_ge(s["consts"], 4)
            pe.wait_ge(s["consts"], 5)

            def misc(use):
                i = MISC[use]
                kind, a = use
                if i >= 1:
                    pe.wait_ge(s["misc_free"], i)
                pb = ps[:, MB, :]
                if kind == "latT":
                    last = nc.tensor.matmul(pb[0:R3, :], w_kv3[:, :], xnT[:, a * L:(a + 1) * L], start=True, stop=True)
                elif kind == "lat":
                    for j in range(TB):
                        t = a * TB + j
                        last = nc.tensor.matmul(pb[:, j * LD:(j + 1) * LD], xnT[:, t * P:(t + 1) * P], w_kv3[:, 0:LD],
                                                start=True, stop=True)
                elif kind == "q":
                    b, g = a
                    last = nc.tensor.matmul(pb, wA[:, g * P:(g + 1) * P], xnT[:, b * L:(b + 1) * L], start=True,
                                            stop=True)
                elif kind == "m":
                    pe.wait_ge(s["mparts_ready"], a + 1)
                    for j in range(TB):
                        last = nc.tensor.transpose(pb[0:2 * HG, j * P:(j + 1) * P],
                                                   mparts[:, a % 2, j, :].bitcast(F32), ident[:, :])
                elif kind == "yt":
                    pe.wait_ge(s["ydrained"], a + 1)
                    for j in range(TB):
                        last = nc.tensor.transpose(pb[:, j * P:(j + 1) * P], ypair[:, a % 2, j * P:(j + 1) * P],
                                                   ident[:, :])
                elif kind == "back":
                    for j in range(TB):
                        last = nc.tensor.transpose(pb[:, j * P:(j + 1) * P], yn[:, a % 2, j, :], ident[:, :])
                else:
                    for j in range(TB):
                        for g in range(G):
                            last = nc.tensor.matmul(pb[:, j * D:(j + 1) * D], ynT[:, g, j * P:(j + 1) * P], wB[:, g, :],
                                                    start=g == 0, stop=g == G - 1)
                last.then_inc(s["misc_full"], 1)

            def scores(u, k):
                b, g = divmod(u, G)
                j, heads = SIT[k]
                nn = NS * u + k
                if k == 0 and g == 0:
                    pe.wait_ge(s[f"qstack{b % 2}"], 16 * 3 * HG * (b // 2 + 1))
                    pe.wait_ge(s["misc_free"], MISC[("latT", b)] + 1)
                if nn >= 2:
                    pe.wait_ge(s["maxed"], nn - 1)
                w = (j + 1) * P
                for m, hh in enumerate(heads):
                    h = g * HG + hh
                    nc.tensor.matmul(ps[:, nn % 2, m * w:(m + 1) * w], qstack[b % 2][0:R3, h, j * P:(j + 1) * P],
                                     lstack[0:R3, b * L:b * L + w], start=True, stop=False)
                    last = nc.tensor.matmul(ps[:, nn % 2, (m + 1) * w - P:(m + 1) * w], identb[:, :], mask_qk[:, :],
                                            start=False, stop=True)
                last.then_inc(s["scores"], 1)

            def scoresT(n):
                u, t = divmod(n, NI)
                b, g = divmod(u, G)
                pair, i = divmod(t, TB)
                w = L - i * P
                if t == 0:
                    pe.wait_ge(s[f"mrow{u % 2}"], 32 * (u // 2 + 1))
                if n >= 2:
                    pe.wait_ge(s["exped"], n - 1)
                for k in range(2):
                    h = g * HG + pair * 2 + k
                    bank = 2 + 2 * (n % 2) + k
                    nc.tensor.matmul(ps[:, bank, 0:w], lstack[:, b * L + i * P:b * L + (i + 1) * P],
                                     qstack[b % 2][:, h, i * P:L], start=True, stop=False)
                    last = nc.tensor.matmul(ps[:, bank, 0:P], identb[:, :], mask_kq[:, :], start=False, stop=True)
                last.then_inc(s["st"], 1)

            def pv(n):
                u, t = divmod(n, NI)
                b, g = divmod(u, G)
                pair, i = divmod(t, TB)
                w = L - i * P
                pe.wait_ge(s["exped"], n + 1)
                if t == 0 and g == 0:
                    pe.wait_ge(s["misc_free"], MISC[("lat", b)] + 1)
                r = 2 * u + pair
                if i == 0 and r >= 1:
                    pe.wait_ge(s["ydrained"], r)
                for k in range(2):
                    last = nc.tensor.matmul(ps[64 * k:64 * k + 2 * LD, YB, i * P:L], laug[:, b * TB + i, :],
                                            probT[:, n % 4, k, 0:w], start=i == 0, stop=i == TB - 1)
                last.then_inc(s["pv"], 1)

            for use in PRO:
                misc(use)
            for u in (0, 1):
                for k in range(NS):
                    scores(u, k)
                misc(("m", u))
            for u in range(NU):
                for t in range(8):
                    n = NI * u + t
                    scoresT(n)
                    if u + 2 < NU:
                        for k in range(FROM[t], FROM[t] + PER[t]):
                            scores(u + 2, k)
                    if n >= 1:
                        pv(n - 1)
                    for use in slot_misc(u, t):
                        misc(use)
            pv(NI * NU - 1)
            for use in EPI:
                misc(use)
            pe.wait_ge(s["misc_free"], len(order))

            pe.wait_ge(s["vback"], 32 * B)
            for t in range(NT + 4):
                if t < NT:
                    pe.wait_ge(s["x2n"], t + 1)
                    if t >= 1:
                        pe.wait_ge(s["x2nT_free"], t)
                    nc.tensor.transpose(ps[:, 0, 0:P], xn[:, t, :], ident[:, :]).then_inc(s["x2nT_full"], 1)
                k = t - 1
                if 0 <= k < NT:
                    pe.wait_ge(s["x2nT_free"], k + 1)
                    if k >= 2:
                        pe.wait_ge(s["csub"], k - 1)
                    for half in range(2):
                        last = nc.tensor.matmul(ps[:, 1 + 2 * (k % 2) + half, 0:KV // 2], xnT[:, k * P:(k + 1) * P],
                                                c_G[:, k // TB, half * (KV // 2):(half + 1) * (KV // 2)],
                                                start=True, stop=True)
                    last.then_inc(s["cscores"], 1)
                k = t - 3
                if 0 <= k < NT:
                    pe.wait_ge(s["pn_ready"], k + 1)
                    if k >= 1:
                        pe.wait_ge(s["cpt_free"], 2 * k)
                    for c in range(KC):
                        w = P if c < KC - 1 else KL
                        last = nc.tensor.transpose(ps[0:w, 5 + c // 4, (c % 4) * P:(c % 4 + 1) * P],
                                                   pr[:, k % 2, c * P:c * P + w], ident[:, :])
                    last.then_inc(s["cpt_full"], 1)
                k = t - 4
                if 0 <= k < NT:
                    pe.wait_ge(s["cpt_free"], 2 * k + 2)
                    if k >= 1:
                        pe.wait_ge(s["cout_free"], k)
                    for c in range(KC):
                        w = P if c < KC - 1 else KL
                        last = nc.tensor.matmul(ps[:, 7, 0:P], pT[0:w, k % 2, c, :], c_V[0:w, k // TB, c, :],
                                                start=c == 0, stop=c == KC - 1)
                    last.then_inc(s["cout_full"], 1)
            pe.wait_ge(s["cout_free"], NT)

            for b in range(B):
                pe.wait_ge(s["f_xn"], TB * (b + 1))
                if b >= 2:
                    pe.wait_ge(s["xT_free"], b - 1)
                for j in range(TB):
                    last = nc.tensor.transpose(ps[:, b % 2, j * P:(j + 1) * P], xn[:, b * TB + j, :], ident[:, :])
                last.then_inc(s["xT_full"], 1)
            pe.wait_ge(s["xT_free"], B)
            pe.wait_ge(s["f_in"], 16)
            for t in range(NT):
                last = nc.tensor.matmul(ps[:, 2, t * E:(t + 1) * E], xnT[:, t * P:(t + 1) * P], w_r[:, :],
                                        start=True, stop=True)
            last.then_inc(s["lg_full"], 1)

            def down(k):
                b, e = divmod(k, NE)
                pe.wait_ge(s["sq_pool"], 2 * (k + 1))
                pe.wait_ge(s["sq_dve"], 2 * (k + 1))
                if k >= 2:
                    pe.wait_ge(s["acc_done"], TB * (k - 1))
                for j in range(TB):
                    for c in range(HC):
                        last = nc.tensor.matmul(ps[:, 6 + k % 2, j * P:(j + 1) * P], hs[:, k % 2, c, j * P:(j + 1) * P],
                                                f_dn[:, k % 2, c, :], start=c == 0, stop=c == HC - 1)
                last.then_inc(s["down_full"], 1)

            for k in range(B * NE):
                b, e = divmod(k, NE)
                pe.wait_ge(s[f"fw{k % 2}"], 32 * (k // 2 + 1))
                for c in range(HC):
                    nn = k * HC + c
                    if nn >= 3:
                        pe.wait_ge(s["relu_done"], nn - 2)
                    nc.tensor.matmul(ps[:, 3 + nn % 3, :], f_up[:, k % 2, c * P:(c + 1) * P], xnT[:, b * L:(b + 1) * L],
                                     start=True, stop=True).then_inc(s["up_full"], 1)
                if k >= 1:
                    down(k - 1)
            down(B * NE - 1)


def kernel(x, ctx_768, L0_attn_Wq, L0_attn_Wkv_down, L0_attn_Wk_up, L0_attn_Wv_up, L0_attn_Wout, L0_xattn_Wq,
           L0_xattn_Wk, L0_xattn_Wv, L0_xattn_Wo, L0_xattn_bo, L0_ffn_W_router, L0_ffn_W_up, L0_ffn_W_down,
           L0_ffn_W_sh_up, L0_ffn_W_sh_down):
    import numpy as np
    import concourse.bacc as bacc
    from concourse.bass_utils import run_bass_kernel_spmd

    def pairs(a):
        h, k, n = a.shape
        return a.reshape(h // 2, 2, k, n).transpose(1, 2, 0, 3).reshape(2 * k, h // 2, n)

    a = {k: np.asarray(v) for k, v in locals().items() if k.startswith("L0") or k in ("x", "ctx_768")}
    ch = a["L0_xattn_Wq"].shape[1] // 64
    d = a["x"].shape[2]
    up = np.concatenate([a["L0_ffn_W_up"], a["L0_ffn_W_sh_up"][None]])
    dn = np.concatenate([a["L0_ffn_W_down"], a["L0_ffn_W_sh_down"][None]])
    ins = {
        "x": a["x"],
        "ctxT": a["ctx_768"].transpose(2, 0, 1),
        "wqT": pairs(a["L0_attn_Wq"].transpose(1, 2, 0)),
        "wkT": pairs(a["L0_attn_Wk_up"].transpose(1, 2, 0)),
        "wvT": pairs(a["L0_attn_Wv_up"].transpose(1, 2, 0)),
        "wout": pairs(a["L0_attn_Wout"]),
        "wkv": a["L0_attn_Wkv_down"],
        "cwqT": pairs(a["L0_xattn_Wq"].T.reshape(ch, 64, d)),
        "cwk": a["L0_xattn_Wk"],
        "cwv": a["L0_xattn_Wv"],
        "cwo": pairs(a["L0_xattn_Wo"].reshape(ch, 64, d)),
        "cbo": np.broadcast_to(a["L0_xattn_bo"], (128, d)),
        "wr": a["L0_ffn_W_router"],
        "wup": up.transpose(1, 0, 2),
        "wdown": dn.reshape(dn.shape[0], -1, 128, d).transpose(2, 0, 1, 3),
    }
    nc = bacc.Bacc("TRN2", target_bir_lowering=False, num_devices=1)
    arrays = {f"in_{k}": np.ascontiguousarray(v) for k, v in ins.items()}
    aps = [nc.dram_tensor(k, v.shape, mybir.dt.from_np(v.dtype), kind="ExternalInput").ap() for k, v in arrays.items()]
    b, sk = a["ctx_768"].shape[:2]
    vscr = nc.dram_tensor("value_scratch", (b, ch, sk, d), F32, kind="Internal").ap()
    out = nc.dram_tensor("out_x", a["x"].shape, F32, kind="ExternalOutput").ap()
    decoder_layer(nc, *aps, vscr, out)
    r = run_bass_kernel_spmd(nc, [arrays], core_ids=[0])
    return r.results[0]["out_x"]
```

```python
from contextlib import ExitStack

import concourse.bass as bass
from concourse import mybir

F32 = mybir.dt.float32
F32R = mybir.dt.float32r
BF16 = mybir.dt.bfloat16
ALU = mybir.AluOpType
ACT = mybir.ActivationFunctionType
AX = mybir.AxisListType

P = 128
EPS = 1e-5
NEG = -1e30


def slot_tiles(tokens, experts):
    return (2 * tokens + experts * (P - 1)) // P


def decoder_layer(nc, x, ctxT, wqT, wkT, wvT, wout, wkv, cwqT, cwk, cwv, cwo, cbo, wr, wup, wdown, vscr, xslot, yslot, out):
    B, L, D = x.shape
    NT = B * L // P
    TB = L // P
    LD = wkv.shape[1]
    HD = 64
    H = wqT.shape[1] * 2
    HG = P // LD
    G = H // HG
    NU = B * G
    CD, SK = ctxT.shape[0], ctxT.shape[2]
    CH = cwqT.shape[1] * 2
    KV = CH * SK
    KC = -(-KV // P)
    KL = KV - (KC - 1) * P
    E = wr.shape[1]
    NE = E + 1
    HC = wup.shape[2] // P
    R3 = 3 * LD
    RM = R3 + 2

    with ExitStack() as ctx:
        def sb(name, shape, dt=F32):
            return ctx.enter_context(nc.sbuf_tensor(name, shape, dt))

        def sem(name):
            return ctx.enter_context(nc.semaphore(name))

        xs = sb("xs", [P, NT, D])
        xn = sb("xn", [P, NT, D])
        xnT = sb("xnT", [P, NT * P])
        ident = sb("ident", [P, P])
        identb = sb("identb", [P, P], BF16)
        mask_qk = sb("mask_qk", [P, P], BF16)
        mask_kq = sb("mask_kq", [P, P], BF16)
        w_qT = sb("w_qT", [P, H // 2, D])
        w_kT = sb("w_kT", [P, H // 2, LD])
        w_vT = sb("w_vT", [P, H // 2, LD])
        w_out = sb("w_out", [P, H // 2, D])
        w_kv3 = sb("w_kv3", [P, R3])
        wA = sb("wA", [P, H * LD])
        wB = sb("wB", [P, G, D])
        c_qT = sb("c_qT", [P, CH // 2, D])
        c_k = sb("c_k", [CD, CH * HD])
        c_v = sb("c_v", [CD, CH * HD])
        c_o = sb("c_o", [P, CH // 2, D])
        c_T = sb("c_T", [CD, B * SK])
        c_bo = sb("c_bo", [P, D])
        c_G = sb("c_G", [P, B, KV])
        c_V1 = sb("c_V1", [SK, 2, 4, D])
        c_V = sb("c_V", [P, B, KC, D])
        w_r = sb("w_r", [P, E])
        stats = sb("stats", [P, NT, 6])
        mv = sb("mv", [P, NT, 2])
        rstd = sb("rstd", [P, NT])
        base = nc.sbuf_base
        big = sb("big", [P, 2 * H * L])
        assert nc.sbuf_base == base + 8 * H * L
        later = [base]

        def sb_later(name, shape, dt=F32):
            size = 4
            for n in shape[1:]:
                size *= n
            t = nc.alloc_sbuf_tensor_at(name, shape, dt, offset=later[0])
            later[0] += size
            assert later[0] <= base + 8 * H * L
            return t

        qstack = [big[0:RM, i * H * L:(i + 1) * H * L].rearrange("p (h t) -> p h t", h=H).bitcast(F32R)
                  for i in range(2)]
        lstack = sb("lstack", [RM, NT * P], F32R)
        laug = sb("laug", [P, NT, 2 * LD])
        qhi = sb("qhi", [P, G, L], F32R)
        qlo = sb("qlo", [P, G, L], F32R)
        c_kT, c_vT = (v[:, :, :].bitcast(F32)[:, 0:CH // 2, 0:B * SK] for v in (qhi, qlo))
        negm = sb("negm", [P, 2, TB, HG])
        mparts = sb("mparts", [P, 2, TB, 2 * HG], F32R)
        mT = sb("mT", [2 * HG, 2, L], F32R)
        probT = sb("probT", [P, 4, 2, L])
        ypair = sb("ypair", [P, 2, L])
        rden = sb("rden", [P, TB, 2])
        yn = sb("yn", [P, 2, TB, P])
        ynT = xn[:, :, :].rearrange("p (g j) d -> p g (j d)", g=G)

        ps = ctx.enter_context(nc.psum_tensor("ps", [P, 8, 512], F32))

        s = {}
        for name in ("x_in w_in cw_in f_in consts lnstat lnroot rootdone xn_ready t_full t_free xnT_ready "
                     "setup_full setup_free vout0 vout1 vback ones_ready "
                     "scores maxed mparts_ready mT_ready mrow0 mrow1 st exped pv ydrained ynormed ynT_ready "
                     "misc_full misc_free qhi_ready qlo_ready lhi_ready llo_ready laug_ready qstack0 qstack1 attn_done "
                     "dchain achain pchain zeroed zfill counts routed sel_ready scat0 scat1 "
                     "x2n x2nT_full x2nT_free cscores csub cexp pn_ready cpt_full cpt_free cout_full cout_free "
                     "cpsum_free f_xn xT_full xT_free lg_full lg_exp lg_done up_full relu_done sq_done down_full acc_done y_out "
                     "gx_full gx_free up_s relu_s hT_s sqr_s dn_s y_ready combined").split() + [
                f"xg{i}" for i in range(4)] + [f"ys{i}" for i in range(4)] + [f"gat{i}" for i in range(16)]:
            s[name] = sem("s_" + name)
        block = ctx.enter_context(nc.Block())

        SIT = [(0, (0, 1, 2, 3)), (1, (0, 1)), (1, (2, 3))] + [(j, (h,)) for j in (2, 3) for h in range(HG)]
        NS = len(SIT)
        PER = [2, 2, 2, 1, 1, 1, 1, 1]
        FROM = [sum(PER[:i]) for i in range(8)]
        NI = 8

        def slot_misc(u, t):
            b, g = divmod(u, G)
            uses = []
            if t == 1 and u >= 1:
                uses.append(("yt", 2 * u - 1))
            if t == 2 and u >= 1:
                uses.append(("back", u - 1))
            if t == 3 and g == 0 and u >= 1:
                uses.append(("out", b - 1))
            if t == 6:
                uses.append(("yt", 2 * u))
            if b + 1 < B:
                for at, use in (((0, 0), ("latT", b + 1)), ((0, 4), ("q", (b + 1, 0))), ((0, 5), ("q", (b + 1, 1))),
                                ((0, 7), ("q", (b + 1, 2))), ((1, 0), ("q", (b + 1, 3))), ((1, 3), ("lat", b + 1))):
                    if at == (g, t):
                        uses.append(use)
            if t == 7 and u + 2 < NU:
                uses.append(("m", u + 2))
            return uses

        PRO = [("latT", 0)] + [("q", (0, g)) for g in range(G)] + [("lat", 0)]
        EPI = [("yt", 2 * NU - 1), ("back", NU - 1), ("out", B - 1)]
        order = PRO + [("m", 0), ("m", 1)]
        for u in range(NU):
            for t in range(8):
                order += slot_misc(u, t)
        order += EPI
        MISC = {use: i for i, use in enumerate(order)}
        MB = 7
        YB = 6
        UPN = HC * B
        HT = NT // 2
        ST = slot_tiles(HT * P, E)
        EW = HC * P

        wait_for = {"x": 16, "w": 16 * 5, "cw": 16 * 6, "f": 16 * 3}

        probf = probT[:, :, :, :].rearrange("p a b n -> p (a b n)")
        f_up = sb_later("f_up", [P, NE, EW])
        f_dn = sb_later("f_dn", [P, NE, HC, D])
        hslot = sb_later("hslot", [P, 2, EW])
        hslotT = sb_later("hslotT", [P, 2, HC, P])
        xslotT = sb_later("xslotT", [P, 2, P])
        ystage = sb_later("ystage", [P, 4, D])
        xg = sb_later("xg", [P, 4, D])
        hs1 = sb_later("hs1", [P, HC, L])
        hs = [qlo[:, :, :].bitcast(F32), hs1[:, :, :]]
        hr = qhi[:, :, :].bitcast(F32)
        yg = probf.rearrange("p (i t c d) -> p i t c d", i=2, t=HT, c=2)
        acc = xs

        sx = probf[:, 0:2 * KV].rearrange("p (i n) -> p i n", i=2)
        pr = probf[:, 2 * KV:4 * KV].rearrange("p (i n) -> p i n", i=2)
        pT = qhi[:, :, :].bitcast(F32).rearrange("p g n -> p (g n)")[:, 0:2 * KC * P].rearrange("p (i c n) -> p i c n", i=2, c=KC)
        cstat = sb("cstat", [P, 2, 3, CH])
        sg = sb("sg", [P, 5, HT, E])
        ltm = sb("ltm", [P, E, E])
        share = sb("share", [P, 2, 2, HT])
        posf = sb("posf", [P, 2, HT])
        posi = sb("posi", [P, 2, 2, HT], mybir.dt.uint32)
        tstat = sb("tstat", [P, 3, E])
        e2 = sb("e2", [P, E, E])
        thr = sb("thr", [P, E, HT])
        sidx = sb("sidx", [P, ST])
        sexp = sb("sexp", [P, ST, E])
        sid = sb("sid", [P, 2, ST])
        sidi = sb("sidi", [P, 2, ST], mybir.dt.int32)
        selb = sb("selb", [P, HT, E], BF16)
        below = sb("below", [P, P], BF16)
        ones = sb("ones", [P, P], BF16)
        ranks = [v.rearrange("p (t e j) -> p t e j", t=2 * HT, e=E)[:, 0:HT] for v in
                 (ypair[:, :, :].rearrange("p i n -> p (i n)"), yn[:, :, :, :].rearrange("p i j n -> p (i j n)"))]

        setup = [("xT", i) for i in range(B)] + [("A", 0), ("A", 1), ("B", 0), ("B", 1)] \
            + [("kT", i) for i in range(CH // 2)] + [("vT", i) for i in range(CH // 2)] + [("G", h) for h in range(CH)] \
            + [("V", i) for i in range(2 * B)]
        SET = {k: i for i, k in enumerate(setup)}
        vset0 = SET[("V", 0)]
        SB = 6

        @block.sync
        def _(sp):
            for b in range(B):
                sp.dma_start(xs[:, b * TB:(b + 1) * TB, :], x[b, :, :].rearrange("(j p) d -> p j d", p=P)
                             ).then_inc(s["x_in"], 16)
            for dst, src in ((w_qT, wqT), (w_kT, wkT), (w_vT, wvT), (w_out, wout)):
                sp.dma_start(dst[:, :, :], src).then_inc(s["w_in"], 16)
            sp.dma_start(w_kv3[:, 0:LD], wkv).then_inc(s["w_in"], 16)
            for dst, src in ((c_k, cwk), (c_v, cwv)):
                sp.dma_start(dst[:, :], src).then_inc(s["cw_in"], 16)
            for dst, src in ((c_qT, cwqT), (c_o, cwo)):
                sp.dma_start(dst[:, :, :], src).then_inc(s["cw_in"], 16)
            sp.dma_start(c_T[:, :], ctxT.rearrange("c b s -> c (b s)")).then_inc(s["cw_in"], 16)
            sp.dma_start(c_bo[:, :], cbo).then_inc(s["cw_in"], 16)

            def stack(b):
                q = qstack[b % 2]
                if b >= 2:
                    sp.wait_ge(s["st"], NI * G * (b - 1))
                for row, part, ready, count in ((0, qhi, "qhi_ready", G * (b + 1)), (LD, qhi, "qhi_ready", G * (b + 1)),
                                                (2 * LD, qlo, "misc_free", MISC[("q", (b, G - 1))] + 1)):
                    sp.wait_ge(s[ready], count)
                    for i in range(HG):
                        dst = q[row:row + LD, :, :].rearrange("p (g i) t -> p g i t", i=HG)[:, :, i, :]
                        sp.dma_start(dst.bitcast(F32), part[i * LD:(i + 1) * LD, :, :].bitcast(F32)).then_inc(s[f"qstack{b % 2}"], 16)

            def mrows(u):
                b, g = divmod(u, G)
                sp.wait_ge(s["misc_free"], MISC[("m", u)] + 1)
                for r in range(2):
                    sp.dma_start(qstack[b % 2][R3 + r:R3 + r + 1, g * HG:(g + 1) * HG, :].bitcast(F32),
                                 mT[r * HG:(r + 1) * HG, u % 2, :].bitcast(F32)).then_inc(s[f"mrow{u % 2}"], 16)

            stack(0)
            mrows(0)
            mrows(1)
            for u in range(NU - 2):
                b, g = divmod(u, G)
                if g == 1 and b + 1 < B:
                    stack(b + 1)
                mrows(u + 2)

            outv = out.rearrange("b (j p) d -> p b j d", p=P)

            sp.wait_ge(s["st"], NI * NU)
            sp.dma_start(w_r[:, :], wr).then_inc(s["f_in"], 16)
            sp.dma_start(f_up[:, :, :], wup).then_inc(s["f_in"], 16)
            sp.dma_start(f_dn[:, :, :, :], wdown).then_inc(s["f_in"], 16)

            def load_slots(n):
                hf, t = divmod(n, ST)
                if t == 0:
                    sp.wait_ge(s[f"scat{hf}"], 32 * HT)
                if n >= 4:
                    sp.wait_ge(s["gx_full"], n - 3)
                sp.dma_start(xg[:, n % 4, :], xslot[hf][t * P:(t + 1) * P, :]).then_inc(s[f"xg{n % 4}"], 16)

            for m in range(2 * ST + 7):
                if m < 2 * ST:
                    load_slots(m)
                n = m - 7
                if n >= 0:
                    hf, t = divmod(n, ST)
                    sp.wait_ge(s["y_ready"], n + 1)
                    sp.dma_start(yslot[hf][t * P:(t + 1) * P, :], ystage[:, n % 4, :]).then_inc(s[f"ys{n % 4}"], 16)
            for b in range(B):
                sp.wait_ge(s["combined"], TB * (b + 1))
                sp.dma_start(outv[:, b, :, :], acc[:, b * TB:(b + 1) * TB, :]).then_inc(s["y_out"], 16)
            sp.wait_ge(s["y_out"], 16 * B)

        @block.gpsimd
        def _(pool):
            chained = [0]

            def chain(ins):
                chained[0] += 1
                ins.then_inc(s["pchain"], 1)
                pool.wait_ge(s["pchain"], chained[0])

            chain(nc.gpsimd.memset(probf[:, 0:ST * D], 0.0))
            for hf in range(2):
                pool.dma_start(xslot[hf].rearrange("(p r) d -> p (r d)", p=P), probf[:, 0:ST * D]
                               ).then_inc(s["zfill"], 16)
            chain(nc.gpsimd.memset(laug[:, :, LD:2 * LD], 1.0))
            chain(nc.gpsimd.memset(lstack[R3:RM, :].bitcast(F32), 1.0))
            chain(nc.gpsimd.memset(ident[:, :], 0.0))
            nc.gpsimd.affine_select(out=ident[:, :], in_=ident[:, :], compare_op=ALU.not_equal, fill=1.0, base=0,
                                    pattern=[[-1, P]], channel_multiplier=1).then_inc(s["consts"], 1)
            pool.wait_ge(s["consts"], 1)
            chain(nc.gpsimd.memset(identb[:, :], 0.0))
            nc.gpsimd.affine_select(out=identb[:, :], in_=identb[:, :], compare_op=ALU.not_equal, fill=1.0, base=0,
                                    pattern=[[-1, P]], channel_multiplier=1).then_inc(s["consts"], 1)
            pool.wait_ge(s["consts"], 2)
            chain(nc.gpsimd.memset(mask_qk[:, :], 0.0))
            nc.gpsimd.affine_select(out=mask_qk[:, :], in_=mask_qk[:, :], compare_op=ALU.is_ge, fill=NEG, base=0,
                                    pattern=[[-1, P]], channel_multiplier=1).then_inc(s["consts"], 1)
            pool.wait_ge(s["consts"], 3)
            chain(nc.gpsimd.memset(mask_kq[:, :], 0.0))
            nc.gpsimd.affine_select(out=mask_kq[:, :], in_=mask_kq[:, :], compare_op=ALU.is_ge, fill=NEG, base=0,
                                    pattern=[[1, P]], channel_multiplier=-1).then_inc(s["consts"], 1)
            pool.wait_ge(s["consts"], 4)
            chain(nc.gpsimd.memset(ltm[:, :, :], 1.0))
            nc.gpsimd.affine_select(out=ltm[:, :, :], in_=ltm[:, :, :], compare_op=ALU.is_gt, fill=0.0, base=0,
                                    pattern=[[1, E], [-1, E]], channel_multiplier=0).then_inc(s["consts"], 1)

            for i in range(2 * B):
                b, half = divmod(i, 2)
                pool.wait_ge(s["setup_free"], vset0 + i + 1)
                pool.dma_start(vscr[b, half:CH:2, :, :].rearrange("h s d -> s h d"),
                             c_V1[:, i % 2, :, :]).then_inc(s[f"vout{i % 2}"], 16)
                if i % 2 == 1:
                    pool.wait_ge(s["vout0"], 16 * (b + 1))
                    pool.wait_ge(s["vout1"], 16 * (b + 1))
                    flat = vscr[b, :, :, :].rearrange("h s d -> (h s) d")
                    pool.dma_start(c_V[:, b, 0:KC - 1, :], flat[0:(KC - 1) * P, :].rearrange("(c p) d -> p c d", p=P)
                                 ).then_inc(s["vback"], 16)
                    pool.dma_start(c_V[0:KL, b, KC - 1, :], flat[(KC - 1) * P:KV, :]).then_inc(s["vback"], 16)

            pool.wait_ge(s["consts"], 5)
            chain(nc.gpsimd.memset(ones[:, :], 1.0))
            chain(nc.gpsimd.memset(below[:, :], 1.0))
            chain(nc.gpsimd.affine_select(out=below[:, :], in_=below[:, :], compare_op=ALU.is_gt, fill=0.0, base=0,
                                          pattern=[[1, P]], channel_multiplier=-1))
            for m in range(HT):
                chain(nc.gpsimd.memset(thr[:, :, m], float(P * m)))
            for t in range(ST):
                ins = nc.gpsimd.memset(sidx[:, t:t + 1], float(t))
                if t < ST - 1:
                    chain(ins)
            ins.then_inc(s["consts"], 1)

            pool.wait_ge(s["zfill"], 32)
            for hf in range(2):
                pool.wait_ge(s["routed"], hf + 1)
                for j in range(HT):
                    for c in range(2):
                        nc.gpsimd.indirect_dma_start(
                            out=xslot[hf], out_offset=bass.IndirectOffsetOnAxis(ap=posi[:, hf, c, j:j + 1], axis=0),
                            in_=xn[:, hf * HT + j, :], in_offset=None).then_inc(s[f"scat{hf}"], 16)
            for hf in range(2):
                last = ST * (hf + 1)
                for i in range(4):
                    pool.wait_ge(s[f"ys{i}"], 16 * len(range(i, last, 4)))
                for j in range(HT):
                    for c in range(2):
                        nc.gpsimd.indirect_dma_start(
                            out=yg[:, hf, j, c, :], out_offset=None, in_=yslot[hf],
                            in_offset=bass.IndirectOffsetOnAxis(ap=posi[:, hf, c, j:j + 1], axis=0)
                        ).then_inc(s[f"gat{hf * HT + j}"], 16)

        @block.scalar
        def _(act):
            def root(k):
                act.wait_ge(s["lnstat"], k + 1)
                nc.scalar.activation(rstd[:, :], rstd[:, :], ACT.Sqrt).then_inc(s["lnroot"], 1)

            root(0)
            for k in setup:
                i = SET[k]
                kind, a = k
                act.wait_ge(s["setup_full"], i + 1)
                pb = ps[:, i % SB, :]
                if kind == "xT":
                    ins = nc.scalar.activation(xnT[:, a * L:(a + 1) * L], pb, ACT.Copy)
                elif kind == "A":
                    ins = nc.scalar.activation(
                        wA[:, :].rearrange("p (h two c) -> p h two c", two=2, c=LD)[:, :, a, :],
                        pb[:, 0:H // 2 * LD].rearrange("p (h c) -> p h c", c=LD), ACT.Copy, scale=float(HD) ** -0.5)
                elif kind == "B":
                    for q in (a * LD, (a + 2) * LD):
                        ins = nc.scalar.activation(wB[q:q + LD, :, :], pb[q:q + LD, :].rearrange(
                            "p (g n) -> p g n", g=G), ACT.Copy)
                elif kind == "kT":
                    ins = nc.scalar.activation(c_kT[:, a, :], pb[:, 0:B * SK], ACT.Copy)
                elif kind == "vT":
                    ins = nc.scalar.activation(c_vT[:, a, :], pb[:, 0:B * SK], ACT.Copy)
                elif kind == "G":
                    ins = nc.scalar.activation(
                        c_G[:, :, a * SK:(a + 1) * SK], pb[:, 0:B * SK].rearrange("p (b s) -> p b s", b=B), ACT.Copy,
                        scale=float(HD) ** -0.5)
                else:
                    if a >= 2:
                        act.wait_ge(s[f"vout{a % 2}"], 16 * (a // 2))
                    ins = nc.scalar.activation(c_V1[:, a % 2, :, :], pb[0:SK, :].rearrange("p (h n) -> p h n", h=4),
                                               ACT.Copy)
                ins.then_inc(s["setup_free"], 1)

            def misc(use):
                i = MISC[use]
                kind, a = use
                pb = ps[:, MB, :]
                if kind == "q":
                    b, g = a
                    act.wait_ge(s["misc_full"], i + 1)
                    if b >= 1 and g == 0:
                        act.wait_ge(s[f"qstack{(b - 1) % 2}"], 16 * 3 * HG * ((b - 1) // 2 + 1))
                    nc.scalar.activation(qhi[:, g, :], pb, ACT.Copy).then_inc(s["qhi_ready"], 1)
                elif kind == "latT":
                    act.wait_ge(s["misc_full"], i + 1)
                    nc.scalar.activation(lstack[0:R3, a * L:(a + 1) * L], pb[0:R3, :], ACT.Copy
                                         ).then_inc(s["lhi_ready"], 1)
                elif kind == "m":
                    act.wait_ge(s["misc_full"], i + 1)
                    if a >= 2:
                        act.wait_ge(s[f"mrow{a % 2}"], 32 * (a // 2))
                    nc.scalar.activation(mT[:, a % 2, :], pb[0:2 * HG, :], ACT.Copy).then_inc(s["misc_free"], 1)
                elif kind == "back":
                    act.wait_ge(s["misc_full"], i + 1)
                    b, g = divmod(a, G)
                    if g == 0 and b >= 1:
                        act.wait_ge(s["misc_full"], MISC[("out", b - 1)] + 1)
                    nc.scalar.activation(ynT[:, g, :], pb, ACT.Copy).then_inc(s["misc_free"], 1)

            def yev(r):
                act.wait_ge(s["pv"], 4 * (r + 1))
                if r >= 2:
                    act.wait_ge(s["misc_full"], MISC[("yt", r - 2)] + 1)
                nc.scalar.activation(ypair[:, r % 2, :], ps[:, YB, :], ACT.Copy).then_inc(s["ydrained"], 1)

            for use in PRO:
                misc(use)
            misc(("m", 0))
            misc(("m", 1))
            act.wait_ge(s["zfill"], 32)
            for u in range(NU):
                for t in range(8):
                    n = NI * u + t
                    pair, i = divmod(t, TB)
                    w = L - i * P
                    act.wait_ge(s["st"], n + 1)
                    if n >= 4:
                        act.wait_ge(s["pv"], n - 3)
                    nc.scalar.activation(probT[:, n % 4, :, 0:w], ps[:, 2 + 2 * (n % 2):4 + 2 * (n % 2), 0:w], ACT.Exp
                                         ).then_inc(s["exped"], 1)
                    if t == 0 and u >= 1:
                        yev(2 * u - 1)
                    if t == 4:
                        yev(2 * u)
                    for use in slot_misc(u, t):
                        misc(use)
            yev(2 * NU - 1)
            misc(EPI[1])

            root(1)
            for t in range(NT + 4):
                if t < NT:
                    act.wait_ge(s["x2nT_full"], t + 1)
                    if t >= 2:
                        act.wait_ge(s["cscores"], t - 1)
                    nc.scalar.activation(xnT[:, t * P:(t + 1) * P], ps[:, 0, 0:P], ACT.Copy).then_inc(s["x2nT_free"], 1)
                k = t - 2
                if 0 <= k < NT:
                    act.wait_ge(s["csub"], k + 1)
                    if k >= 2:
                        act.wait_ge(s["pn_ready"], k - 1)
                    nc.scalar.activation(pr[:, k % 2, :], sx[:, k % 2, :], ACT.Exp).then_inc(s["cexp"], 1)
                k = t - 3
                if 0 <= k < NT:
                    act.wait_ge(s["cpt_full"], k + 1)
                    if k >= 2:
                        act.wait_ge(s["cout_full"], k - 1)
                    nc.scalar.activation(pT[:, k % 2, 0:4, :], ps[:, 5, :].rearrange("p (c n) -> p c n", c=4), ACT.Copy
                                         ).then_inc(s["cpt_free"], 1)
                    nc.scalar.activation(pT[0:KL, k % 2, 4, :], ps[0:KL, 6, 0:P], ACT.Copy).then_inc(s["cpt_free"], 1)

            root(2)
            for b in range(B):
                act.wait_ge(s["xT_full"], b + 1)
                nc.scalar.activation(xnT[:, b * L:(b + 1) * L], ps[:, b % 2, :], ACT.Copy).then_inc(s["xT_free"], 1)
            for hf in range(2):
                act.wait_ge(s["lg_full"], hf + 1)
                nc.scalar.activation(sg[:, 0, :, :], ps[:, 2, hf * P:hf * P + HT * E].rearrange("p (t e) -> p t e", e=E),
                                     ACT.Exp, scale=-1.0).then_inc(s["lg_exp"], 1)
                if hf == 0:
                    act.wait_ge(s["routed"], 1)

            def shared(b):
                for n in range(HC * b, HC * (b + 1)):
                    act.wait_ge(s["relu_done"], n + 1)
                    if b >= 2:
                        act.wait_ge(s["down_full"], b - 1)
                    nc.scalar.activation(hs[b % 2][:, n % HC, :], hr[:, n % 4, :], ACT.Square).then_inc(s["sq_done"], 1)

            shared(0)
            shared(1)
            for n in range(2 * ST + 2):
                if n < 2 * ST:
                    act.wait_ge(s["gx_full"], n + 1)
                    if n >= 2:
                        act.wait_ge(s["up_s"], n - 1)
                    nc.scalar.activation(xslotT[:, n % 2, :], ps[:, n % 2, 0:P], ACT.Copy).then_inc(s["gx_free"], 1)
                k = n - 2
                if k >= 0:
                    act.wait_ge(s["hT_s"], k + 1)
                    if k >= 2:
                        act.wait_ge(s["dn_s"], k - 1)
                    nc.scalar.activation(hslotT[:, k % 2, :, :], ps[:, 4 + k % 2, :].rearrange("p (c n) -> p c n", c=HC),
                                         ACT.Square).then_inc(s["sqr_s"], 1)
            shared(2)
            shared(3)

        @block.vector
        def _(dve):
            chained = [0]

            def chain(ins):
                chained[0] += 1
                ins.then_inc(s["dchain"], 1)
                dve.wait_ge(s["dchain"], chained[0])

            def norm_stats(k):
                for t in range(NT):
                    if t < NT - 1:
                        nc.vector.bn_stats(stats[:, t, :], xs[:, t, :])
                    else:
                        chain(nc.vector.bn_stats(stats[:, t, :], xs[:, t, :]))
                for t in range(NT):
                    if t < NT - 1:
                        nc.vector.bn_aggr(mv[:, t, :], stats[:, t, :])
                    else:
                        chain(nc.vector.bn_aggr(mv[:, t, :], stats[:, t, :]))
                nc.vector.tensor_scalar_add(rstd[:, :], mv[:, :, 1], EPS).then_inc(s["lnstat"], 1)
                dve.wait_ge(s["lnroot"], k + 1)
                chain(nc.vector.reciprocal(rstd[:, :], rstd[:, :]))

            def norm(t):
                return nc.vector.tensor_scalar(xn[:, t, :], xs[:, t, :], mv[:, t, 0:1], rstd[:, t:t + 1],
                                               ALU.subtract, ALU.mult)

            dve.wait_ge(s["w_in"], 80)
            for r in (1, 2):
                chain(nc.vector.tensor_copy(w_kv3[:, r * LD:(r + 1) * LD], w_kv3[:, 0:LD]))
            dve.wait_ge(s["x_in"], 16 * B)
            norm_stats(0)
            for t in range(NT):
                norm(t).then_inc(s["xn_ready"], 1)

            def maxes(u, k):
                j, heads = SIT[k]
                nn = NS * u + k
                dve.wait_ge(s["scores"], nn + 1)
                if u >= 2 and k == 0:
                    dve.wait_ge(s["mparts_ready"], u - 1)
                w = (j + 1) * P
                nh = len(heads)
                nc.vector.tensor_reduce(negm[:, u % 2, j, heads[0]:heads[0] + nh],
                                        ps[:, nn % 2, 0:nh * w].rearrange("p (h n) -> p h n", h=nh), AX.X, ALU.max,
                                        negate=True).then_inc(s["maxed"], 1)

            def split_max(u):
                dve.wait_ge(s["maxed"], NS * (u + 1))
                if u >= 2:
                    dve.wait_ge(s["misc_full"], MISC[("m", u - 2)] + 1)
                chain(nc.vector.tensor_copy(mparts[:, u % 2, :, 0:HG], negm[:, u % 2, :, :]))
                nc.vector.tensor_tensor(mparts[:, u % 2, :, HG:2 * HG], negm[:, u % 2, :, :],
                                        mparts[:, u % 2, :, 0:HG].bitcast(F32), ALU.subtract
                                        ).then_inc(s["mparts_ready"], 1)

            def misc(use):
                i = MISC[use]
                kind, a = use
                pb = ps[:, MB, :]
                if kind == "q":
                    b, g = a
                    dve.wait_ge(s["qhi_ready"], G * b + g + 1)
                    nc.vector.tensor_tensor(qlo[:, g, :], pb, qhi[:, g, :].bitcast(F32), ALU.subtract
                                            ).then_inc(s["misc_free"], 1)
                elif kind == "latT":
                    dve.wait_ge(s["lhi_ready"], a + 1)
                    nc.vector.tensor_tensor(lstack[LD:2 * LD, a * L:(a + 1) * L], pb[LD:2 * LD, :],
                                            lstack[LD:2 * LD, a * L:(a + 1) * L].bitcast(F32), ALU.subtract
                                            ).then_inc(s["misc_free"], 1)
                elif kind == "lat":
                    dve.wait_ge(s["misc_full"], i + 1)
                    nc.vector.tensor_copy(laug[:, a * TB:(a + 1) * TB, 0:LD],
                                          pb[:, 0:TB * LD].rearrange("p (j c) -> p j c", j=TB)
                                          ).then_inc(s["misc_free"], 1)
                elif kind == "yt":
                    dve.wait_ge(s["misc_full"], i + 1)
                    v = pb.rearrange("p (j h c) -> p j h c", j=TB, h=2)
                    chain(nc.vector.reciprocal(rden[:, :, :], v[:, :, :, LD]))
                    u, half = divmod(a, 2)
                    if u >= 2 and half == 0:
                        dve.wait_ge(s["misc_full"], MISC[("back", u - 2)] + 1)
                    nc.vector.tensor_tensor(
                        yn[:, u % 2, :, half * 2 * LD:(half + 1) * 2 * LD].rearrange("p j (h c) -> p j h c", h=2),
                        v[:, :, :, 0:LD], rden[:, :, :].unsqueeze(3).broadcast_to([P, TB, 2, LD]), ALU.mult
                    ).then_inc(s["misc_free"], 1)
                elif kind == "out":
                    dve.wait_ge(s["misc_full"], i + 1)
                    nc.vector.tensor_tensor(xs[:, a * TB:(a + 1) * TB, :], pb.rearrange("p (j n) -> p j n", j=TB),
                                            xs[:, a * TB:(a + 1) * TB, :], ALU.add).then_inc(s["misc_free"], 1)

            for use in PRO:
                misc(use)
            for u in (0, 1):
                for k in range(NS):
                    maxes(u, k)
                split_max(u)
            for u in range(NU):
                for t in range(8):
                    if u + 2 < NU:
                        for k in range(FROM[t], FROM[t] + PER[t]):
                            maxes(u + 2, k)
                        if t == 7:
                            split_max(u + 2)
                    for use in slot_misc(u, t):
                        misc(use)
            misc(EPI[0])
            misc(EPI[2])
            dve.wait_ge(s["misc_free"], len(order))

            norm_stats(1)
            dve.wait_ge(s["cw_in"], 96)
            for t in range(NT + 4):
                if t < NT:
                    norm(t).then_inc(s["x2n"], 1)
                k = t - 1
                if 0 <= k < NT:
                    dve.wait_ge(s["cscores"], k + 1)
                    sc = ps[:, 1 + 2 * (k % 2):3 + 2 * (k % 2), 0:KV // 2].rearrange("p a (h s) -> p a h s", s=SK)
                    mx = cstat[:, k % 2, 0, :].rearrange("p (a h) -> p a h", a=2)
                    chain(nc.vector.tensor_reduce(mx, sc, AX.X, ALU.max))
                    if k >= 2:
                        dve.wait_ge(s["cexp"], k - 1)
                    nc.vector.tensor_tensor(
                        sx[:, k % 2, :].rearrange("p (a h s) -> p a h s", a=2, s=SK), sc,
                        mx.unsqueeze(3).broadcast_to([P, 2, CH // 2, SK]), ALU.subtract).then_inc(s["csub"], 1)
                k = t - 2
                if 0 <= k < NT:
                    dve.wait_ge(s["cexp"], k + 1)
                    pv = pr[:, k % 2, :].rearrange("p (h s) -> p h s", s=SK)
                    chain(nc.vector.tensor_reduce(cstat[:, k % 2, 1, :], pv, AX.X, ALU.add))
                    chain(nc.vector.reciprocal(cstat[:, k % 2, 2, :], cstat[:, k % 2, 1, :]))
                    nc.vector.tensor_tensor(pv, pv, cstat[:, k % 2, 2, :].unsqueeze(2).broadcast_to([P, CH, SK]),
                                            ALU.mult).then_inc(s["pn_ready"], 1)
                k = t - 4
                if 0 <= k < NT:
                    chain(nc.vector.tensor_tensor(xs[:, k, :], xs[:, k, :], c_bo[:, :], ALU.add))
                    dve.wait_ge(s["cout_full"], k + 1)
                    nc.vector.tensor_tensor(xs[:, k, :], ps[:, 7, 0:P], xs[:, k, :], ALU.add
                                            ).then_inc(s["cout_free"], 1)
            dve.wait_ge(s["cout_free"], NT)

            norm_stats(2)
            for t in range(NT):
                norm(t).then_inc(s["f_xn"], 1)
            dve.wait_ge(s["consts"], 6)

            def route(hf):
                dve.wait_ge(s["lg_exp"], hf + 1)
                prob, oh1, oh2, tmp, tmp2 = (sg[:, i, :, :] for i in range(5))
                chain(nc.vector.tensor_scalar_add(tmp, prob, 1.0))
                chain(nc.vector.reciprocal(prob, tmp))
                pj = prob.unsqueeze(2).broadcast_to([P, HT, E, E])
                pe_ = prob.unsqueeze(3).broadcast_to([P, HT, E, E])
                chain(nc.vector.tensor_tensor(ranks[0], pj, pe_, ALU.is_equal))
                chain(nc.vector.tensor_tensor(ranks[0], ranks[0], ltm[:, :, :].unsqueeze(1).broadcast_to([P, HT, E, E]),
                                              ALU.mult))
                chain(nc.vector.tensor_tensor(ranks[1], pj, pe_, ALU.is_gt))
                chain(nc.vector.tensor_tensor(ranks[0], ranks[0], ranks[1], ALU.add))
                chain(nc.vector.tensor_reduce(tmp, ranks[0], AX.X, ALU.add))
                chain(nc.vector.tensor_single_scalar(selb[:, :, :], tmp, 1.5, ALU.is_lt))
                nc.vector.tensor_single_scalar(oh1, tmp, 0.0, ALU.is_equal).then_inc(s["sel_ready"], 1)
                chain(nc.vector.tensor_single_scalar(oh2, tmp, 1.0, ALU.is_equal))
                dve.wait_ge(s["sel_ready"], hf + 1)
                for c, oh in enumerate((oh1, oh2)):
                    chain(nc.vector.tensor_tensor(tmp, prob, oh, ALU.mult))
                    chain(nc.vector.tensor_reduce(share[:, hf, c, :], tmp, AX.X, ALU.add))
                chain(nc.vector.tensor_tensor(posf[:, 0, :], share[:, hf, 0, :], share[:, hf, 1, :], ALU.add))
                chain(nc.vector.tensor_scalar_add(posf[:, 0, :], posf[:, 0, :], 1e-6))
                chain(nc.vector.reciprocal(posf[:, 1, :], posf[:, 0, :]))
                for c in range(2):
                    chain(nc.vector.tensor_tensor(share[:, hf, c, :], share[:, hf, c, :], posf[:, 1, :], ALU.mult))
                dve.wait_ge(s["counts"], hf + 1)
                pre = ps[:, 2, hf * P:hf * P + HT * E]
                cnt = ps[:, 2, hf * P + HT * E:hf * P + (HT + 1) * E]
                tiles, first, through = (tstat[:, i, :] for i in range(3))
                chain(nc.vector.tensor_tensor(e2[:, :, 0:HT], cnt.unsqueeze(2).broadcast_to([P, E, HT]), thr[:, :, :],
                                              ALU.is_gt))
                chain(nc.vector.tensor_reduce(tiles, e2[:, :, 0:HT], AX.X, ALU.add))
                chain(nc.vector.tensor_tensor(e2[:, :, :], tiles.unsqueeze(1).broadcast_to([P, E, E]), ltm[:, :, :],
                                              ALU.mult))
                chain(nc.vector.tensor_reduce(first, e2[:, :, :], AX.X, ALU.add))
                chain(nc.vector.tensor_tensor(through, first, tiles, ALU.add))
                chain(nc.vector.tensor_scalar(first, first, float(P), None, ALU.mult))
                chain(nc.vector.tensor_tensor(tmp2, pre.rearrange("p (t e) -> p t e", e=E),
                                              first.unsqueeze(1).broadcast_to([P, HT, E]), ALU.add))
                for c, oh in enumerate((oh1, oh2)):
                    chain(nc.vector.tensor_tensor(tmp, tmp2, oh, ALU.mult))
                    chain(nc.vector.tensor_reduce(posf[:, c, :], tmp, AX.X, ALU.add))
                chain(nc.vector.tensor_copy(posi[:, hf, :, :], posf[:, :, :]))
                chain(nc.vector.tensor_tensor(sexp[:, :, :], through.unsqueeze(1).broadcast_to([P, ST, E]),
                                              sidx[:, :].unsqueeze(2).broadcast_to([P, ST, E]), ALU.is_le))
                chain(nc.vector.tensor_reduce(sid[:, hf, :], sexp[:, :, :], AX.X, ALU.add))
                chain(nc.vector.tensor_scalar(sid[:, hf, :], sid[:, hf, :], float(E - 1), None, ALU.min))
                nc.vector.tensor_copy(sidi[:, hf, :], sid[:, hf, :]).then_inc(s["routed"], 1)
                dve.wait_ge(s["routed"], hf + 1)

            def shared(b):
                for n in range(HC * b, HC * (b + 1)):
                    dve.wait_ge(s["up_full"], n + 1)
                    if n >= 4:
                        dve.wait_ge(s["sq_done"], n - 3)
                    nc.vector.tensor_scalar(hr[:, n % 4, :], ps[:, 3 + n % 3, :], 0.0, None, ALU.max
                                            ).then_inc(s["relu_done"], 1)

            def shared_add(b):
                dve.wait_ge(s["down_full"], b + 1)
                nc.vector.tensor_tensor(acc[:, b * TB:(b + 1) * TB, :], ps[:, 6 + b % 2, :].rearrange(
                    "p (j n) -> p j n", j=TB), acc[:, b * TB:(b + 1) * TB, :], ALU.add).then_inc(s["acc_done"], 1)

            def combine(t):
                hf, j = divmod(t, HT)
                dve.wait_ge(s["acc_done"], t // TB + 1)
                dve.wait_ge(s[f"gat{t}"], 32)
                chain(nc.vector.scalar_tensor_tensor(acc[:, t, :], yg[:, hf, j, 0, :], share[:, hf, 0, j:j + 1],
                                                     acc[:, t, :], ALU.mult, ALU.add))
                nc.vector.scalar_tensor_tensor(acc[:, t, :], yg[:, hf, j, 1, :], share[:, hf, 1, j:j + 1],
                                               acc[:, t, :], ALU.mult, ALU.add).then_inc(s["combined"], 1)

            route(0)
            route(1)
            for step in (shared, shared_add):
                for b in (0, 1):
                    step(b)
            for n in range(2 * ST + 3):
                k = n - 1
                if 0 <= k < 2 * ST:
                    dve.wait_ge(s["up_s"], k + 1)
                    if k >= 2:
                        dve.wait_ge(s["hT_s"], k - 1)
                    nc.vector.tensor_scalar(hslot[:, k % 2, :], ps[:, 2 + k % 2, :], 0.0, None, ALU.max
                                            ).then_inc(s["relu_s"], 1)
                k = n - 3
                if k >= 0:
                    dve.wait_ge(s["dn_s"], k + 1)
                    if k >= 4:
                        dve.wait_ge(s[f"ys{k % 4}"], 16 * (k // 4))
                    nc.vector.tensor_copy(ystage[:, k % 4, :], ps[:, 6 + k % 2, 0:D]).then_inc(s["y_ready"], 1)
                    if k >= 2 * ST - HT - 1 and k - (2 * ST - HT - 1) < HT:
                        combine(k - (2 * ST - HT - 1))
            for step in (shared, shared_add):
                for b in (2, 3):
                    step(b)
            for t in range(HT, NT):
                combine(t)

        @block.tensor
        def _(pe):
            pe.wait_ge(s["consts"], 1)
            for k in setup:
                i = SET[k]
                kind, a = k
                if i >= SB:
                    pe.wait_ge(s["setup_free"], i - SB + 1)
                bank = i % SB
                if kind == "xT":
                    pe.wait_ge(s["xn_ready"], TB * (a + 1))
                    for j in range(TB):
                        last = nc.tensor.transpose(ps[:, bank, j * P:(j + 1) * P], xn[:, a * TB + j, :], ident[:, :])
                elif kind == "A":
                    pe.wait_ge(s["w_in"], 80)
                    r = a * HD
                    for i in range(H // 2):
                        last = nc.tensor.matmul(ps[:, bank, i * LD:(i + 1) * LD], w_qT[r:r + HD, i, :],
                                                w_kT[r:r + HD, i, :], start=True, stop=True)
                elif kind == "B":
                    r = a * HD
                    for h in range(a, H, 2):
                        q = (h % HG) * LD
                        last = nc.tensor.matmul(ps[q:q + LD, bank, (h // HG) * D:(h // HG + 1) * D],
                                                w_vT[r:r + HD, h // 2, :], w_out[r:r + HD, h // 2, :],
                                                start=True, stop=True)
                elif kind in ("kT", "vT"):
                    pe.wait_ge(s["cw_in"], 96)
                    w = c_k if kind == "kT" else c_v
                    last = nc.tensor.matmul(ps[:, bank, 0:B * SK], w[:, a * P:(a + 1) * P], c_T[:, :],
                                            start=True, stop=True)
                elif kind == "G":
                    r = (a % 2) * HD
                    pe.wait_ge(s["setup_free"], SET[("kT", a // 2)] + 1)
                    last = nc.tensor.matmul(ps[:, bank, 0:B * SK], c_qT[r:r + HD, a // 2, :], c_kT[r:r + HD, a // 2, :],
                                            start=True, stop=True)
                else:
                    b, half = divmod(a, 2)
                    pe.wait_ge(s["setup_free"], SET[("vT", CH // 2 - 1)] + 1)
                    r = half * HD
                    for hh in range(4):
                        h = 2 * hh + half
                        last = nc.tensor.matmul(ps[0:SK, bank, hh * D:(hh + 1) * D],
                                                c_vT[r:r + HD, h // 2, b * SK:(b + 1) * SK],
                                                c_o[r:r + HD, h // 2, :], start=True, stop=True)
                last.then_inc(s["setup_full"], 1)
            pe.wait_ge(s["setup_free"], len(setup))
            pe.wait_ge(s["consts"], 4)
            pe.wait_ge(s["consts"], 5)

            def misc(use):
                i = MISC[use]
                kind, a = use
                if i >= 1:
                    pe.wait_ge(s["misc_free"], i)
                pb = ps[:, MB, :]
                if kind == "latT":
                    last = nc.tensor.matmul(pb[0:R3, :], w_kv3[:, :], xnT[:, a * L:(a + 1) * L], start=True, stop=True)
                elif kind == "lat":
                    for j in range(TB):
                        t = a * TB + j
                        last = nc.tensor.matmul(pb[:, j * LD:(j + 1) * LD], xnT[:, t * P:(t + 1) * P], w_kv3[:, 0:LD],
                                                start=True, stop=True)
                elif kind == "q":
                    b, g = a
                    last = nc.tensor.matmul(pb, wA[:, g * P:(g + 1) * P], xnT[:, b * L:(b + 1) * L], start=True,
                                            stop=True)
                elif kind == "m":
                    pe.wait_ge(s["mparts_ready"], a + 1)
                    for j in range(TB):
                        last = nc.tensor.transpose(pb[0:2 * HG, j * P:(j + 1) * P],
                                                   mparts[:, a % 2, j, :].bitcast(F32), ident[:, :])
                elif kind == "yt":
                    pe.wait_ge(s["ydrained"], a + 1)
                    for j in range(TB):
                        last = nc.tensor.transpose(pb[:, j * P:(j + 1) * P], ypair[:, a % 2, j * P:(j + 1) * P],
                                                   ident[:, :])
                elif kind == "back":
                    for j in range(TB):
                        last = nc.tensor.transpose(pb[:, j * P:(j + 1) * P], yn[:, a % 2, j, :], ident[:, :])
                else:
                    for j in range(TB):
                        for g in range(G):
                            last = nc.tensor.matmul(pb[:, j * D:(j + 1) * D], ynT[:, g, j * P:(j + 1) * P], wB[:, g, :],
                                                    start=g == 0, stop=g == G - 1)
                last.then_inc(s["misc_full"], 1)

            def scores(u, k):
                b, g = divmod(u, G)
                j, heads = SIT[k]
                nn = NS * u + k
                if k == 0 and g == 0:
                    pe.wait_ge(s[f"qstack{b % 2}"], 16 * 3 * HG * (b // 2 + 1))
                    pe.wait_ge(s["misc_free"], MISC[("latT", b)] + 1)
                if nn >= 2:
                    pe.wait_ge(s["maxed"], nn - 1)
                w = (j + 1) * P
                for m, hh in enumerate(heads):
                    h = g * HG + hh
                    nc.tensor.matmul(ps[:, nn % 2, m * w:(m + 1) * w], qstack[b % 2][0:R3, h, j * P:(j + 1) * P],
                                     lstack[0:R3, b * L:b * L + w], start=True, stop=False)
                    last = nc.tensor.matmul(ps[:, nn % 2, (m + 1) * w - P:(m + 1) * w], identb[:, :], mask_qk[:, :],
                                            start=False, stop=True)
                last.then_inc(s["scores"], 1)

            def scoresT(n):
                u, t = divmod(n, NI)
                b, g = divmod(u, G)
                pair, i = divmod(t, TB)
                w = L - i * P
                if t == 0:
                    pe.wait_ge(s[f"mrow{u % 2}"], 32 * (u // 2 + 1))
                if n >= 2:
                    pe.wait_ge(s["exped"], n - 1)
                for k in range(2):
                    h = g * HG + pair * 2 + k
                    bank = 2 + 2 * (n % 2) + k
                    nc.tensor.matmul(ps[:, bank, 0:w], lstack[:, b * L + i * P:b * L + (i + 1) * P],
                                     qstack[b % 2][:, h, i * P:L], start=True, stop=False)
                    last = nc.tensor.matmul(ps[:, bank, 0:P], identb[:, :], mask_kq[:, :], start=False, stop=True)
                last.then_inc(s["st"], 1)

            def pv(n):
                u, t = divmod(n, NI)
                b, g = divmod(u, G)
                pair, i = divmod(t, TB)
                w = L - i * P
                pe.wait_ge(s["exped"], n + 1)
                if t == 0 and g == 0:
                    pe.wait_ge(s["misc_free"], MISC[("lat", b)] + 1)
                r = 2 * u + pair
                if i == 0 and r >= 1:
                    pe.wait_ge(s["ydrained"], r)
                for k in range(2):
                    last = nc.tensor.matmul(ps[64 * k:64 * k + 2 * LD, YB, i * P:L], laug[:, b * TB + i, :],
                                            probT[:, n % 4, k, 0:w], start=i == 0, stop=i == TB - 1)
                last.then_inc(s["pv"], 1)

            for use in PRO:
                misc(use)
            for u in (0, 1):
                for k in range(NS):
                    scores(u, k)
                misc(("m", u))
            for u in range(NU):
                for t in range(8):
                    n = NI * u + t
                    scoresT(n)
                    if u + 2 < NU:
                        for k in range(FROM[t], FROM[t] + PER[t]):
                            scores(u + 2, k)
                    if n >= 1:
                        pv(n - 1)
                    for use in slot_misc(u, t):
                        misc(use)
            pv(NI * NU - 1)
            for use in EPI:
                misc(use)
            pe.wait_ge(s["misc_free"], len(order))

            pe.wait_ge(s["vback"], 32 * B)
            for t in range(NT + 4):
                if t < NT:
                    pe.wait_ge(s["x2n"], t + 1)
                    if t >= 1:
                        pe.wait_ge(s["x2nT_free"], t)
                    nc.tensor.transpose(ps[:, 0, 0:P], xn[:, t, :], ident[:, :]).then_inc(s["x2nT_full"], 1)
                k = t - 1
                if 0 <= k < NT:
                    pe.wait_ge(s["x2nT_free"], k + 1)
                    if k >= 2:
                        pe.wait_ge(s["csub"], k - 1)
                    for half in range(2):
                        last = nc.tensor.matmul(ps[:, 1 + 2 * (k % 2) + half, 0:KV // 2], xnT[:, k * P:(k + 1) * P],
                                                c_G[:, k // TB, half * (KV // 2):(half + 1) * (KV // 2)],
                                                start=True, stop=True)
                    last.then_inc(s["cscores"], 1)
                k = t - 3
                if 0 <= k < NT:
                    pe.wait_ge(s["pn_ready"], k + 1)
                    if k >= 1:
                        pe.wait_ge(s["cpt_free"], 2 * k)
                    for c in range(KC):
                        w = P if c < KC - 1 else KL
                        last = nc.tensor.transpose(ps[0:w, 5 + c // 4, (c % 4) * P:(c % 4 + 1) * P],
                                                   pr[:, k % 2, c * P:c * P + w], ident[:, :])
                    last.then_inc(s["cpt_full"], 1)
                k = t - 4
                if 0 <= k < NT:
                    pe.wait_ge(s["cpt_free"], 2 * k + 2)
                    if k >= 1:
                        pe.wait_ge(s["cout_free"], k)
                    for c in range(KC):
                        w = P if c < KC - 1 else KL
                        last = nc.tensor.matmul(ps[:, 7, 0:P], pT[0:w, k % 2, c, :], c_V[0:w, k // TB, c, :],
                                                start=c == 0, stop=c == KC - 1)
                    last.then_inc(s["cout_full"], 1)
            pe.wait_ge(s["cout_free"], NT)

            for b in range(B):
                pe.wait_ge(s["f_xn"], TB * (b + 1))
                if b >= 2:
                    pe.wait_ge(s["xT_free"], b - 1)
                for j in range(TB):
                    last = nc.tensor.transpose(ps[:, b % 2, j * P:(j + 1) * P], xn[:, b * TB + j, :], ident[:, :])
                last.then_inc(s["xT_full"], 1)
            pe.wait_ge(s["xT_free"], B)
            pe.wait_ge(s["f_in"], 48)
            pe.wait_ge(s["consts"], 6)
            for hf in range(2):
                if hf:
                    pe.wait_ge(s["routed"], 1)
                for j in range(HT):
                    t = hf * HT + j
                    last = nc.tensor.matmul(ps[:, 2, hf * P + j * E:hf * P + (j + 1) * E], xnT[:, t * P:(t + 1) * P],
                                            w_r[:, :], start=True, stop=True)
                last.then_inc(s["lg_full"], 1)
                pe.wait_ge(s["sel_ready"], hf + 1)
                for j in range(HT):
                    for i in range(j + 1):
                        nc.tensor.matmul(ps[:, 2, hf * P + j * E:hf * P + (j + 1) * E],
                                         below[:, :] if i == j else ones[:, :], selb[:, i, :], start=i == 0, stop=i == j)
                for i in range(HT):
                    last = nc.tensor.matmul(ps[:, 2, hf * P + HT * E:hf * P + (HT + 1) * E], ones[:, :], selb[:, i, :],
                                            start=i == 0, stop=i == HT - 1)
                last.then_inc(s["counts"], 1)

            def shared_up(b):
                for n in range(HC * b, HC * (b + 1)):
                    if n >= 3:
                        pe.wait_ge(s["relu_done"], n - 2)
                    nc.tensor.matmul(ps[:, 3 + n % 3, :], f_up[:, NE - 1, (n % HC) * P:(n % HC + 1) * P],
                                     xnT[:, b * L:(b + 1) * L], start=True, stop=True).then_inc(s["up_full"], 1)

            def shared_down(b):
                pe.wait_ge(s["sq_done"], HC * (b + 1))
                for j in range(TB):
                    for c in range(HC):
                        last = nc.tensor.matmul(ps[:, 6 + b % 2, j * P:(j + 1) * P], hs[b % 2][:, c, j * P:(j + 1) * P],
                                                f_dn[:, NE - 1, c, :], start=c == 0, stop=c == HC - 1)
                last.then_inc(s["down_full"], 1)

            def shared(b0):
                shared_up(b0)
                shared_up(b0 + 1)
                shared_down(b0)
                shared_down(b0 + 1)

            shared(0)
            pe.wait_ge(s["acc_done"], 2)
            pe.wait_ge(s["relu_done"], 2 * HC)
            experts = {}
            for n in range(2 * ST + 3):
                if n < 2 * ST:
                    hf, t = divmod(n, ST)
                    experts[n] = nc.tensor.value_load(sidi[0:1, hf, t:t + 1], min_val=0, max_val=E - 1)
                    pe.wait_ge(s[f"xg{n % 4}"], 16 * (n // 4 + 1))
                    if n >= 2:
                        pe.wait_ge(s["gx_free"], n - 1)
                    nc.tensor.transpose(ps[:, n % 2, 0:P], xg[:, n % 4, :], ident[:, :]).then_inc(s["gx_full"], 1)
                k = n - 1
                if 0 <= k < 2 * ST:
                    hf, t = divmod(k, ST)
                    pe.wait_ge(s["gx_free"], k + 1)
                    if k >= 2:
                        pe.wait_ge(s["relu_s"], k - 1)
                    e = experts[k]
                    nc.tensor.matmul(ps[:, 2 + k % 2, :], xslotT[:, k % 2, :], f_up[:, bass.ds(e, 1), :].rearrange(
                        "p a n -> p (a n)"), start=True, stop=True).then_inc(s["up_s"], 1)
                k = n - 2
                if 0 <= k < 2 * ST:
                    pe.wait_ge(s["relu_s"], k + 1)
                    if k >= 2:
                        pe.wait_ge(s["sqr_s"], k - 1)
                    for c in range(HC):
                        last = nc.tensor.transpose(ps[:, 4 + k % 2, c * P:(c + 1) * P], hslot[:, k % 2, c * P:(c + 1) * P],
                                                   ident[:, :])
                    last.then_inc(s["hT_s"], 1)
                k = n - 3
                if k >= 0:
                    hf, t = divmod(k, ST)
                    pe.wait_ge(s["sqr_s"], k + 1)
                    if k >= 2:
                        pe.wait_ge(s["y_ready"], k - 1)
                    e = experts[k]
                    for c in range(HC):
                        last = nc.tensor.matmul(ps[:, 6 + k % 2, 0:D], hslotT[:, k % 2, c, :],
                                                f_dn[:, bass.ds(e, 1), c, :].rearrange("p a n -> p (a n)"),
                                                start=c == 0, stop=c == HC - 1)
                    last.then_inc(s["dn_s"], 1)
            pe.wait_ge(s["y_ready"], 2 * ST)
            pe.wait_ge(s["sqr_s"], 2 * ST)
            shared(2)


def kernel(x, ctx_768, L0_attn_Wq, L0_attn_Wkv_down, L0_attn_Wk_up, L0_attn_Wv_up, L0_attn_Wout, L0_xattn_Wq,
           L0_xattn_Wk, L0_xattn_Wv, L0_xattn_Wo, L0_xattn_bo, L0_ffn_W_router, L0_ffn_W_up, L0_ffn_W_down,
           L0_ffn_W_sh_up, L0_ffn_W_sh_down):
    import numpy as np
    import concourse.bacc as bacc
    from concourse.bass_utils import run_bass_kernel_spmd

    def pairs(a):
        h, k, n = a.shape
        return a.reshape(h // 2, 2, k, n).transpose(1, 2, 0, 3).reshape(2 * k, h // 2, n)

    a = {k: np.asarray(v) for k, v in locals().items() if k.startswith("L0") or k in ("x", "ctx_768")}
    ch = a["L0_xattn_Wq"].shape[1] // 64
    d = a["x"].shape[2]
    up = np.concatenate([a["L0_ffn_W_up"], a["L0_ffn_W_sh_up"][None]])
    dn = np.concatenate([a["L0_ffn_W_down"], a["L0_ffn_W_sh_down"][None]])
    ins = {
        "x": a["x"],
        "ctxT": a["ctx_768"].transpose(2, 0, 1),
        "wqT": pairs(a["L0_attn_Wq"].transpose(1, 2, 0)),
        "wkT": pairs(a["L0_attn_Wk_up"].transpose(1, 2, 0)),
        "wvT": pairs(a["L0_attn_Wv_up"].transpose(1, 2, 0)),
        "wout": pairs(a["L0_attn_Wout"]),
        "wkv": a["L0_attn_Wkv_down"],
        "cwqT": pairs(a["L0_xattn_Wq"].T.reshape(ch, 64, d)),
        "cwk": a["L0_xattn_Wk"],
        "cwv": a["L0_xattn_Wv"],
        "cwo": pairs(a["L0_xattn_Wo"].reshape(ch, 64, d)),
        "cbo": np.broadcast_to(a["L0_xattn_bo"], (128, d)),
        "wr": a["L0_ffn_W_router"],
        "wup": up.transpose(1, 0, 2),
        "wdown": dn.reshape(dn.shape[0], -1, 128, d).transpose(2, 0, 1, 3),
    }
    nc = bacc.Bacc("TRN2", target_bir_lowering=False, num_devices=1)
    arrays = {f"in_{k}": np.ascontiguousarray(v) for k, v in ins.items()}
    aps = [nc.dram_tensor(k, v.shape, mybir.dt.from_np(v.dtype), kind="ExternalInput").ap() for k, v in arrays.items()]
    b, sk = a["ctx_768"].shape[:2]
    vscr = nc.dram_tensor("value_scratch", (b, ch, sk, d), F32, kind="Internal").ap()
    ns = slot_tiles(x.shape[0] * x.shape[1] // 2, a["L0_ffn_W_router"].shape[1]) * 128
    xslot = [nc.dram_tensor(f"x_slots{i}", (ns, d), F32, kind="Internal").ap() for i in range(2)]
    yslot = [nc.dram_tensor(f"y_slots{i}", (ns, d), F32, kind="Internal").ap() for i in range(2)]
    out = nc.dram_tensor("out_x", a["x"].shape, F32, kind="ExternalOutput").ap()
    decoder_layer(nc, *aps, vscr, xslot, yslot, out)
    r = run_bass_kernel_spmd(nc, [arrays], core_ids=[0])
    return r.results[0]["out_x"]
```

```python
from contextlib import ExitStack

import concourse.bass as bass
from concourse import mybir

F32 = mybir.dt.float32
F32R = mybir.dt.float32r
BF16 = mybir.dt.bfloat16
ALU = mybir.AluOpType
ACT = mybir.ActivationFunctionType
AX = mybir.AxisListType

P = 128
EPS = 1e-5
NEG = -1e30


def slot_tiles(tokens, experts):
    return (2 * tokens + experts * (P - 1)) // P


def decoder_layer(nc, x, ctxT, wqT, wkT, wvT, wout, wkv, cwqT, cwk, cwv, cwo, cbo, wr, wup, wdown, vscr, xslot,
                  yslot, out):
    B, L, D = x.shape
    NT = B * L // P
    TB = L // P
    LD = wkv.shape[1]
    HD = 64
    H = wqT.shape[1] * 2
    HG = P // LD
    G = H // HG
    NU = B * G
    CD, SK = ctxT.shape[0], ctxT.shape[2]
    CH = cwqT.shape[1] * 2
    KV = CH * SK
    KC = -(-KV // P)
    KL = KV - (KC - 1) * P
    E = wr.shape[1]
    NE = E + 1
    HC = wup.shape[2] // P
    R3 = 3 * LD
    RM = R3 + 2

    with ExitStack() as ctx:
        def sb(name, shape, dt=F32):
            return ctx.enter_context(nc.sbuf_tensor(name, shape, dt))

        def sem(name):
            return ctx.enter_context(nc.semaphore(name))

        xs = sb("xs", [P, NT, D])
        xn = sb("xn", [P, NT, D])
        xnT = sb("xnT", [P, NT * P])
        ident = sb("ident", [P, P])
        identb = sb("identb", [P, P], BF16)
        mask_qk = sb("mask_qk", [P, P], BF16)
        early = sb("early", [P, 8 * L])

        def early_part(first, *shape):
            n = shape[0] * shape[1]
            return early[:, first:first + n].rearrange("p (a n) -> p a n", a=shape[0])

        w_qT = early_part(0, H // 2, D)
        w_kT = sb("w_kT", [P, H // 2, LD])
        w_vT = sb("w_vT", [P, H // 2, LD])
        w_out = early_part(2 * L, H // 2, D)
        w_kv3 = sb("w_kv3", [P, R3])
        wA = sb("wA", [P, H * LD])
        wB = sb("wB", [P, G, D])
        prob_sums = early[:, :].rearrange("p (u h n) -> p u h n", u=2, h=HG)
        c_T = sb("c_T", [CD, B * SK])
        c_bo = sb("c_bo", [P, D])
        c_G = sb("c_G", [P, B, KV])
        c_V = sb("c_V", [P, B, KC, D])
        w_r = sb("w_r", [P, E])
        stats = sb("stats", [P, NT, 6])
        mv = sb("mv", [P, NT, 2])
        rstd = sb("rstd", [P, NT])
        base = nc.sbuf_base
        big = sb("big", [P, 2 * H * L])
        assert nc.sbuf_base == base + 8 * H * L
        later = {"even": base, "all": base}

        def sb_later(name, shape, dt=F32, over="all"):
            size = 4
            for n in shape[1:]:
                size *= n
            t = nc.alloc_sbuf_tensor_at(name, shape, dt, offset=later[over])
            later[over] += size
            assert later[over] <= base + (8 if over == "all" else 4) * H * L
            return t

        c_qT = sb_later("c_qT", [P, CH // 2, D], over="even")
        c_o = sb_later("c_o", [P, CH // 2, D], over="even")
        c_k = sb_later("c_k", [CD, CH * HD], over="even")
        c_v = sb_later("c_v", [CD, CH * HD], over="even")
        c_kT = sb_later("c_kT", [P, CH // 2, B * SK], over="even")
        c_vT = sb_later("c_vT", [P, CH // 2, B * SK], over="even")
        c_V1 = sb_later("c_V1", [SK, 4, 4, D], over="even")

        qstack = [big[0:RM, i * H * L:(i + 1) * H * L].rearrange("p (h t) -> p h t", h=H).bitcast(F32R)
                  for i in range(2)]
        lstack = sb("lstack", [RM, NT * P], F32R)
        latent = sb("latent", [P, NT, LD])
        to_rows = sb("to_rows", [P, TB, LD])
        from_rows = sb("from_rows", [P, TB, P])
        rden = sb("rden", [P, 2, P])
        qhi = sb("qhi", [P, G, L], F32R)
        qlo = sb("qlo", [P, G, L], F32R)
        neg_max = sb("negm", [P, 2, TB, HG])
        max_parts = sb("mparts", [P, 2, TB, 2 * HG], F32R)
        max_rows = sb("mT", [2 * HG, 2, L], F32R)
        PIECES = 6
        probT = sb("probT", [P, PIECES, 2, L])
        yraw = sb("yraw", [P, 2, L])
        ynT = sb("ynT", [P, G, L])

        ps = ctx.enter_context(nc.psum_tensor("ps", [P, 8, 512], F32))

        s = {}
        for names in (
                "x0_in x_in wA_in wkv_in wB_in cross_w_in router_w_in ffn_w_in qstack_first qstack0 qstack1 max_rows0 max_rows1 slot_x_in0 slot_x_in1 slot_x_in2 slot_x_in3",
                "values_out0 values_out1 values_out2 values_out3 values_back slot_y_out0 slot_y_out1 slot_y_out2 slot_y_out3 y_out",
                "pool_order consts slots_zeroed scattered0 scattered1",
                "var_ready std_ready xn_ready x2_rstd_ready x2n_ready x3n_ready",
                "setup_full setup_free csetup_full csetup_free latent_w_ready",
                "scores_ready max_ready max_parts_ready",
                "scoresT_ready probs_ready probs_masked",
                "sums_begun sums_added sums_ready",
                "outputs_ready outputs_drained",
                "misc_full misc_free qhi_ready latT_hi_ready",
                "x2nT_full x2nT_free cross_scores_ready cross_shifted cross_exp_ready cross_rsum_ready",
                "cross_probs_ready residual_biased cross_probsT_full cross_probsT_free cross_out_full cross_out_free",
                "x3nT_full x3nT_free logits_ready logits_exp_ready choice_ready counts_ready slots_ready",
                "shared_up_ready shared_relu_ready shared_hidden_ready shared_down_ready shared_added",
                "slot_xT_full slot_xT_free slot_weights_ready slot_up_ready slot_relu_ready slot_hidden_ready slot_down_ready slot_y_ready combined",
                "vector_order"):
            for name in names.split():
                s[name] = sem("s_" + name)
        for t in range(NT):
            s[f"gathered{t}"] = sem(f"s_gathered{t}")
        block = ctx.enter_context(nc.Block())

        SCORE_TILES = [(0, (0, 1, 2, 3)), (1, (0, 1)), (1, (2, 3))] + [(j, (h,)) for j in (2, 3) for h in range(HG)]
        NS = len(SCORE_TILES)
        PER = [1, 0, 2, 2, 0, 2, 2, 2]
        LEAD = 8

        def score_bank(n):
            return n % 6 if n < NS + LEAD else n % 2

        def score_tiles(u, t):
            lo = NS * (u + 1) + LEAD + sum(PER[:t])
            return [divmod(n, NS) for n in range(lo, min(lo + PER[t], NS * NU))]

        ITEMS = 8

        MAXES_AT = 4

        def slot_misc(u, t):
            b, g = divmod(u, G)
            uses = []
            if t == 2 and u >= 1:
                uses.append(("den", u - 1))
            if t == MAXES_AT and u + 1 < NU:
                uses.append(("m", u + 1))
            if t == 5 and u >= 1:
                uses.append(("spread", u - 1))
            if t == 0 and g == 1 and b >= 1:
                uses.append(("out", b - 1))
            if b + 1 < B:
                for at, use in (((0, 0), ("latT", b + 1)), ((0, 3), ("q", (b + 1, 0))), ((0, 5), ("q", (b + 1, 1))),
                                ((0, 6), ("q", (b + 1, 2))), ((0, 7), ("q", (b + 1, 3))), ((1, 3), ("lat", b + 1))):
                    if at == (g, t):
                        uses.append(use)
            return uses

        FIRST_USES = [("latT", 0)] + [("q", (0, g)) for g in range(G)] + [("lat", 0)]
        LAST_USES = [("den", NU - 1), ("spread", NU - 1), ("out", B - 1)]
        order = FIRST_USES + [("m", 0)]
        for u in range(NU):
            for t in range(8):
                order += slot_misc(u, t)
        order += LAST_USES
        MISC = {use: i for i, use in enumerate(order)}
        MISC_BANK = 7
        TRANSPOSE_BANK, LOGIT_BANK = (0, 0, 0, 1), (0, 7)
        OUT_BANK = 6

        def misc_bank(i):
            return ps[:, OUT_BANK if i < len(FIRST_USES) and i % 2 else MISC_BANK, :]

        HT = NT // 2
        ST = slot_tiles(HT * P, E)
        EW = HC * P

        probf = probT[:, :, :, :].rearrange("p a b n -> p (a b n)")
        f_up = sb_later("f_up", [P, NE, EW])
        f_dn = sb_later("f_dn", [P, NE, HC, D])
        hslot = sb_later("hslot", [P, 2, HC, P])
        hslotT = sb_later("hslotT", [P, 2, HC, P])
        f_upE = sb_later("f_upE", [P, 2, EW])
        xslotT = sb_later("xslotT", [P, 2, P])
        ystage = sb_later("ystage", [P, 4, D])
        xg = sb_later("xg", [P, 4, D])
        hs1 = sb_later("hs1", [P, HC, L])
        shared_h = [qlo[:, :, :].bitcast(F32), hs1[:, :, :]]
        shared_relu_buf = qhi[:, :, :].bitcast(F32)
        gathered_y = probf[:, 0:2 * HT * 2 * D].rearrange("p (i t c d) -> p i t c d", i=2, t=HT, c=2)
        acc = xs

        cross_shift = probf[:, 0:2 * KV].rearrange("p (i n) -> p i n", i=2)
        cross_p = probf[:, 2 * KV:5 * KV].rearrange("p (i n) -> p i n", i=3)
        cross_pT = qhi[:, :, :].bitcast(F32).rearrange("p g n -> p (g n)")[:, 0:2 * KC * P].rearrange(
            "p (i c n) -> p i c n", i=2, c=KC)
        cstat = sb("cstat", [P, 2, 3, CH])
        route_tmp = sb("sg", [P, 5, HT, E])
        lower = sb("ltm", [P, E, E])
        share = sb("share", [P, 2, 2, HT])
        posf = sb("posf", [P, 2, HT])
        posi = sb("posi", [P, 2, 2, HT], mybir.dt.uint32)
        tstat = sb("tstat", [P, 3, E])
        pairs_tmp = sb("e2", [P, E, E])
        tile_bounds = sb("thr", [P, E, HT])
        tile_index = sb("sidx", [P, ST])
        tile_past = sb("sexp", [P, ST, E])
        tile_expert_f = sb("sid", [P, 2, ST])
        tile_expert = sb("sidi", [P, 2, ST], mybir.dt.int32)
        chosen = sb("selb", [P, HT, E], BF16)
        below = sb("below", [P, P], BF16)
        ones = sb("ones", [P, P], BF16)
        first_of = sb("first_of", [P, E])

        setup = [("A", 0), ("A", 1), ("xT", 0)]
        setup1 = len(setup)
        setup += [("xT", i) for i in range(1, B)] + [("B", 0), ("B", 1)]
        SETUP = {k: i for i, k in enumerate(setup)}
        csetup = [("kT", i) for i in range(CH // 2)] + [("vT", i) for i in range(CH // 2)] \
            + [("V", i) for i in range(2 * B)] + [("G", h) for h in range(CH)]
        CSETUP = {k: i for i, k in enumerate(csetup)}

        last_score = max((u, t) for u in range(NU) for t in range(8) if score_tiles(u, t))

        def slot_csetup(u, t):
            first = ITEMS * last_score[0] + last_score[1] + 1
            m, slots, n = ITEMS * u + t - first, ITEMS * NU - first, len(csetup)
            return csetup[m * n // slots:(m + 1) * n // slots] if m >= 0 else []

        SETUP_BANKS = 6
        ROOTS = [(0, TB), (TB, NT), (0, NT - TB), (NT - TB, NT), (0, HT), (HT, NT)]

        @block.sync
        def _(sp):
            def load_x(b, name):
                sp.dma_start(xs[:, b * TB:(b + 1) * TB, :], x[b, :, :].rearrange("(j p) d -> p j d", p=P)
                             ).then_inc(s[name], 16)

            load_x(0, "x0_in")
            for dst, src in ((w_qT, wqT), (w_kT, wkT)):
                sp.dma_start(dst[:, :, :], src).then_inc(s["wA_in"], 16)
            sp.dma_start(w_kv3[:, 0:LD], wkv).then_inc(s["wkv_in"], 16)
            for b in range(1, B):
                load_x(b, "x_in")
            for dst, src in ((w_vT, wvT), (w_out, wout)):
                sp.dma_start(dst[:, :, :], src).then_inc(s["wB_in"], 16)

            def stack(b):
                if b >= 2:
                    sp.wait_ge(s["scoresT_ready"], ITEMS * G * (b - 1))
                groups = [(0, 1, "qstack_first"), (1, G, "qstack0")] if b == 0 else [(0, G, f"qstack{b % 2}")]
                for lo, hi, done in groups:
                    stack_groups(b, lo, hi, done)

            def stack_groups(b, lo, hi, done):
                q = qstack[b % 2]
                for row, part, ready, count in ((0, qhi, "qhi_ready", G * b + hi), (LD, qhi, "qhi_ready", G * b + hi),
                                                (2 * LD, qlo, "misc_free", MISC[("q", (b, hi - 1))] + 1)):
                    sp.wait_ge(s[ready], count)
                    for i in range(HG):
                        dst = q[row:row + LD, :, :].rearrange("p (g i) t -> p g i t", i=HG)[:, lo:hi, i, :]
                        sp.dma_start(dst.bitcast(F32), part[i * LD:(i + 1) * LD, lo:hi, :].bitcast(F32)
                                     ).then_inc(s[done], 16)

            def mrows(u):
                b, g = divmod(u, G)
                sp.wait_ge(s["misc_free"], MISC[("m", u)] + 1)
                for r in range(2):
                    sp.dma_start(qstack[b % 2][R3 + r:R3 + r + 1, g * HG:(g + 1) * HG, :].bitcast(F32),
                                 max_rows[r * HG:(r + 1) * HG, u % 2, :].bitcast(F32)).then_inc(s[f"max_rows{u % 2}"], 16)

            stack(0)
            mrows(0)
            for u in range(NU - 1):
                b, g = divmod(u, G)
                mrows(u + 1)
                if g == 0 and b + 1 < B:
                    stack(b + 1)
                if u == NU - G:
                    sp.wait_ge(s["scoresT_ready"], ITEMS * (NU - G))
                    for dst, src in ((c_k, cwk), (c_v, cwv)):
                        sp.dma_start(dst[:, :], src).then_inc(s["cross_w_in"], 16)
                    for dst, src in ((c_qT, cwqT), (c_o, cwo)):
                        sp.dma_start(dst[:, :, :], src).then_inc(s["cross_w_in"], 16)
                    sp.dma_start(c_T[:, :], ctxT.rearrange("c b s -> c (b s)")).then_inc(s["cross_w_in"], 16)
                    sp.dma_start(c_bo[:, :], cbo).then_inc(s["cross_w_in"], 16)

            for i in range(2 * B):
                b, half = divmod(i, 2)
                sp.wait_ge(s["csetup_free"], CSETUP[("V", i)] + 1)
                sp.dma_start(vscr[b, half:CH:2, :, :].rearrange("h s d -> s h d"),
                             c_V1[:, i % 4, :, :]).then_inc(s[f"values_out{i % 4}"], 16)
            for b in range(B):
                for i in (2 * b, 2 * b + 1):
                    sp.wait_ge(s[f"values_out{i % 4}"], 16 * (i // 4 + 1))
                flat = vscr[b, :, :, :].rearrange("h s d -> (h s) d")
                sp.dma_start(c_V[:, b, 0:KC - 1, :], flat[0:(KC - 1) * P, :].rearrange("(c p) d -> p c d", p=P)
                             ).then_inc(s["values_back"], 16)
                sp.dma_start(c_V[0:KL, b, KC - 1, :], flat[(KC - 1) * P:KV, :]).then_inc(s["values_back"], 16)

            outv = out.rearrange("b (j p) d -> p b j d", p=P)

            sp.wait_ge(s["scoresT_ready"], ITEMS * NU)
            sp.wait_ge(s["csetup_full"], len(csetup))
            sp.dma_start(w_r[:, :], wr).then_inc(s["router_w_in"], 16)
            sp.dma_start(f_up[:, :, :], wup).then_inc(s["ffn_w_in"], 16)
            sp.dma_start(f_dn[:, :, :, :], wdown).then_inc(s["ffn_w_in"], 16)

            def load_slots(n):
                hf, t = divmod(n, ST)
                if t == 0:
                    sp.wait_ge(s[f"scattered{hf}"], 32 * HT)
                if n >= 4:
                    sp.wait_ge(s["slot_xT_full"], n - 3)
                sp.dma_start(xg[:, n % 4, :], xslot[hf][t * P:(t + 1) * P, :]).then_inc(s[f"slot_x_in{n % 4}"], 16)

            for m in range(2 * ST + 7):
                if m < 2 * ST:
                    load_slots(m)
                n = m - 7
                if n >= 0:
                    hf, t = divmod(n, ST)
                    sp.wait_ge(s["slot_y_ready"], n + 1)
                    sp.dma_start(yslot[hf][t * P:(t + 1) * P, :], ystage[:, n % 4, :]).then_inc(s[f"slot_y_out{n % 4}"], 16)
            for b in range(B):
                sp.wait_ge(s["combined"], TB * (b + 1))
                sp.wait_ge(s["shared_added"], b + 1)
                sp.dma_start(outv[:, b, :, :], acc[:, b * TB:(b + 1) * TB, :]).then_inc(s["y_out"], 16)
            sp.wait_ge(s["y_out"], 16 * B)

        @block.gpsimd
        def _(pool):
            chained = [0]

            def chain(ins):
                chained[0] += 1
                ins.then_inc(s["pool_order"], 1)
                pool.wait_ge(s["pool_order"], chained[0])

            chain(nc.gpsimd.memset(lstack[R3:RM, :].bitcast(F32), 1.0))
            chain(nc.gpsimd.memset(ident[:, :], 0.0))
            nc.gpsimd.affine_select(out=ident[:, :], in_=ident[:, :], compare_op=ALU.not_equal, fill=1.0, base=0,
                                    pattern=[[-1, P]], channel_multiplier=1).then_inc(s["consts"], 1)
            pool.wait_ge(s["consts"], 1)
            chain(nc.gpsimd.memset(probf[:, 0:ST * D], 0.0))
            for hf in range(2):
                pool.dma_start(xslot[hf].rearrange("(p r) d -> p (r d)", p=P), probf[:, 0:ST * D]
                               ).then_inc(s["slots_zeroed"], 16)
            chain(nc.gpsimd.memset(identb[:, :], 0.0))
            nc.gpsimd.affine_select(out=identb[:, :], in_=identb[:, :], compare_op=ALU.not_equal, fill=1.0, base=0,
                                    pattern=[[-1, P]], channel_multiplier=1).then_inc(s["consts"], 1)
            pool.wait_ge(s["consts"], 2)
            chain(nc.gpsimd.memset(mask_qk[:, :], 0.0))
            nc.gpsimd.affine_select(out=mask_qk[:, :], in_=mask_qk[:, :], compare_op=ALU.is_ge, fill=NEG, base=0,
                                    pattern=[[-1, P]], channel_multiplier=1).then_inc(s["consts"], 1)
            pool.wait_ge(s["consts"], 3)
            chain(nc.gpsimd.memset(lower[:, :, :], 1.0))
            nc.gpsimd.affine_select(out=lower[:, :, :], in_=lower[:, :, :], compare_op=ALU.is_gt, fill=0.0, base=0,
                                    pattern=[[1, E], [-1, E]], channel_multiplier=0).then_inc(s["consts"], 1)

            chain(nc.gpsimd.memset(to_rows[:, :, :], 0.0))
            for j in range(TB):
                chain(nc.gpsimd.memset(to_rows[:, j, j:LD:TB], 1.0))
            chain(nc.gpsimd.memset(from_rows[:, :, :], 0.0))
            chain(nc.gpsimd.affine_select(out=from_rows[:, :, :], in_=from_rows[:, :, :], compare_op=ALU.not_equal,
                                          fill=1.0, base=0, pattern=[[-1, TB], [-LD, HG], [0, LD]],
                                          channel_multiplier=1))
            pool.wait_ge(s["consts"], 4)
            chain(nc.gpsimd.memset(ones[:, :], 1.0))
            chain(nc.gpsimd.memset(below[:, :], 1.0))
            chain(nc.gpsimd.affine_select(out=below[:, :], in_=below[:, :], compare_op=ALU.is_gt, fill=0.0, base=0,
                                          pattern=[[1, P]], channel_multiplier=-1))
            for m in range(HT):
                chain(nc.gpsimd.memset(tile_bounds[:, :, m], float(P * m)))
            for e in range(E):
                chain(nc.gpsimd.memset(first_of[:, e:e + 1], float(E - e)))
            for t in range(ST):
                ins = nc.gpsimd.memset(tile_index[:, t:t + 1], float(t))
                if t < ST - 1:
                    chain(ins)
            ins.then_inc(s["consts"], 1)

            def add_up(u, t):
                i, pair = divmod(t, 2)
                n = ITEMS * u + t
                added = 4 * u + t - 2
                pool.wait_ge(s["probs_masked"], n + 1)
                total = prob_sums[:, u % 2, 2 * pair:2 * pair + 2, i * P:L]
                if i == 1:
                    if u >= 2:
                        pool.wait_ge(s["misc_full"], MISC[("den", u - 2)] + 1)
                    first = probT[:, (n - 2) % PIECES, :, P:L]
                else:
                    pool.wait_ge(s["sums_added"], added - 1)
                    first = total
                nc.gpsimd.tensor_tensor(total, first, probT[:, n % PIECES, :, 0:L - i * P], ALU.add).then_inc(s["sums_added"], 1)

            def norm2(t):
                if t in (0, NT - TB):
                    pool.wait_ge(s["x2_rstd_ready"], 1 if t == 0 else 2)
                nc.gpsimd.tensor_scalar(xn[:, t, :], xs[:, t, :], mv[:, t, 0:1], rstd[:, t:t + 1], ALU.subtract, ALU.mult
                                        ).then_inc(s["x2n_ready"], 1)

            AHEAD = 5
            for u in range(NU):
                for t in range(ITEMS):
                    n = ITEMS * u + t
                    pool.wait_ge(s["probs_ready"], n + 1)
                    nc.gpsimd.affine_select(out=probT[:, n % PIECES, :, 0:P], in_=probT[:, n % PIECES, :, 0:P],
                                            compare_op=ALU.is_ge, fill=0.0, base=0, pattern=[[0, 2], [1, P]],
                                            channel_multiplier=-1).then_inc(s["probs_masked"], 1)
                    if t in (3, 4, 5, 6):
                        add_up(u, t - 1)
                    if u == NU - 1 and t < AHEAD:
                        norm2(t)

            def scatter(hf, n):
                j, c = divmod(n, 2)
                nc.gpsimd.indirect_dma_start(
                    out=xslot[hf], out_offset=bass.IndirectOffsetOnAxis(ap=posi[:, hf, c, j:j + 1], axis=0),
                    in_=xn[:, hf * HT + j, :], in_offset=None).then_inc(s[f"scattered{hf}"], 16)

            pool.wait_ge(s["cross_w_in"], 96)
            scattered = 0
            for k in range(NT):
                pool.wait_ge(s["cross_rsum_ready"], k + 1)
                v = cross_p[:, k % 3, :].rearrange("p (h s) -> p h s", s=SK)
                nc.gpsimd.tensor_tensor(v, v, cstat[:, k % 2, 2, :].unsqueeze(2).broadcast_to([P, CH, SK]), ALU.mult
                                        ).then_inc(s["cross_probs_ready"], 1)
                pool.wait_ge(s["x2n_ready"], k + 1)
                nc.gpsimd.tensor_tensor(xs[:, k, :], xs[:, k, :], c_bo[:, :], ALU.add).then_inc(s["residual_biased"], 1)
                if k + AHEAD < NT:
                    norm2(k + AHEAD)
                if k >= HT + 6:
                    if k == HT + 6:
                        pool.wait_ge(s["slots_zeroed"], 32)
                        pool.wait_ge(s["slots_ready"], 1)
                    for n in range(scattered, scattered + 2):
                        scatter(0, n)
                    scattered += 2
            for n in range(scattered, 2 * HT):
                scatter(0, n)
            pool.wait_ge(s["slots_ready"], 2)
            for n in range(2 * HT):
                scatter(1, n)
            for hf in range(2):
                last = ST * (hf + 1)
                for i in range(4):
                    pool.wait_ge(s[f"slot_y_out{i}"], 16 * len(range(i, last, 4)))
                for j in range(HT):
                    for c in range(2):
                        nc.gpsimd.indirect_dma_start(
                            out=gathered_y[:, hf, j, c, :], out_offset=None, in_=yslot[hf],
                            in_offset=bass.IndirectOffsetOnAxis(ap=posi[:, hf, c, j:j + 1], axis=0)
                        ).then_inc(s[f"gathered{hf * HT + j}"], 16)

        @block.scalar
        def _(act):
            def root(k):
                lo, hi = ROOTS[k]
                r = rstd[:, lo:hi]
                act.wait_ge(s["var_ready"], k + 1)
                nc.scalar.activation(r, r, ACT.Sqrt).then_inc(s["std_ready"], 1)

            def evacuate(k):
                i = SETUP[k]
                kind, a = k
                act.wait_ge(s["setup_full"], i + 1)
                pb = ps[:, i % SETUP_BANKS, :]
                if kind == "xT":
                    ins = nc.scalar.activation(xnT[:, a * L:(a + 1) * L], pb, ACT.Copy)
                elif kind == "A":
                    ins = nc.scalar.activation(
                        wA[:, :].rearrange("p (h two c) -> p h two c", two=2, c=LD)[:, :, a, :],
                        pb[:, 0:H // 2 * LD].rearrange("p (h c) -> p h c", c=LD), ACT.Copy, scale=float(HD) ** -0.5)
                else:
                    for q in (a * LD, (a + 2) * LD):
                        ins = nc.scalar.activation(wB[q:q + LD, :, :], pb[q:q + LD, :].rearrange(
                            "p (g n) -> p g n", g=G), ACT.Copy)
                ins.then_inc(s["setup_free"], 1)

            root(0)
            root(1)
            for k in setup[:setup1]:
                evacuate(k)

            def misc(use):
                i = MISC[use]
                kind, a = use
                pb = misc_bank(i)
                if kind == "q":
                    b, g = a
                    act.wait_ge(s["misc_full"], i + 1)
                    if b == 1 and g == 0:
                        act.wait_ge(s["qstack_first"], 16 * 3 * HG)
                    if b >= 1 and g == 0:
                        act.wait_ge(s[f"qstack{(b - 1) % 2}"], 16 * 3 * HG * ((b - 1) // 2 + 1))
                    nc.scalar.activation(qhi[:, g, :], pb, ACT.Copy).then_inc(s["qhi_ready"], 1)
                elif kind == "latT":
                    act.wait_ge(s["misc_full"], i + 1)
                    nc.scalar.activation(lstack[0:R3, a * L:(a + 1) * L], pb[0:R3, :], ACT.Copy
                                         ).then_inc(s["latT_hi_ready"], 1)
                elif kind == "m":
                    act.wait_ge(s["misc_full"], i + 1)
                    if a >= 2:
                        act.wait_ge(s[f"max_rows{a % 2}"], 32 * (a // 2))
                    nc.scalar.activation(max_rows[:, a % 2, :], pb[0:2 * HG, :], ACT.Copy).then_inc(s["misc_free"], 1)

            def yev(u):
                act.wait_ge(s["outputs_ready"], TB * (u + 1))
                if u >= 2:
                    act.wait_ge(s["misc_free"], MISC[("spread", u - 2)] + 1)
                nc.scalar.activation(yraw[:, u % 2, :], ps[:, OUT_BANK, :], ACT.Copy).then_inc(s["outputs_drained"], 1)

            for use in FIRST_USES:
                misc(use)
            for k in setup[setup1:]:
                evacuate(k)
            misc(("m", 0))
            act.wait_ge(s["slots_zeroed"], 32)
            for u in range(NU):
                for t in range(8):
                    n = ITEMS * u + t
                    w = L - t // 2 * P
                    act.wait_ge(s["scoresT_ready"], n + 1)
                    if n >= PIECES:
                        v, r = divmod(n - PIECES, ITEMS)
                        act.wait_ge(s["outputs_ready"], (n - PIECES) // 2 + 1)
                        if r < 2:
                            act.wait_ge(s["sums_begun"], 2 * v + r + 1)
                            act.wait_ge(s["sums_added"], 4 * v + r + 1)
                        elif r < 6:
                            act.wait_ge(s["sums_added"], 4 * v + r - 1)
                        else:
                            act.wait_ge(s["sums_ready"], 2 * v + r - 5)
                    nc.scalar.activation(probT[:, n % PIECES, :, 0:w], ps[:, 2 + 2 * (n % 2):4 + 2 * (n % 2), 0:w], ACT.Exp
                                         ).then_inc(s["probs_ready"], 1)
                    if t == 2 and u >= 1:
                        yev(u - 1)
                    if t in (2, 3):
                        act.wait_ge(s["probs_masked"], n - 1)
                        if u >= 2 and t == 2:
                            act.wait_ge(s["misc_full"], MISC[("den", u - 2)] + 1)
                        nc.scalar.activation(prob_sums[:, u % 2, 2 * (t - 2):2 * (t - 1), 0:P], probT[:, (n - 2) % PIECES, :, 0:P],
                                             ACT.Copy).then_inc(s["sums_begun"], 1)
                    for use in slot_misc(u, t):
                        misc(use)
                    if u == NU - 3 and t == 5:
                        root(2)
            yev(NU - 1)

            def logits(hf):
                for b in (2 * hf, 2 * hf + 1):
                    act.wait_ge(s["x3nT_full"], b + 1)
                    nc.scalar.activation(xnT[:, b * L:(b + 1) * L], ps[:, TRANSPOSE_BANK[b], :], ACT.Copy).then_inc(s["x3nT_free"], 1)
                act.wait_ge(s["logits_ready"], hf + 1)
                if hf == 1:
                    act.wait_ge(s["slots_ready"], 1)
                nc.scalar.activation(route_tmp[:, 0, :, :], ps[:, LOGIT_BANK[hf], hf * P:hf * P + HT * E].rearrange(
                    "p (t e) -> p t e", e=E), ACT.Exp, scale=-1.0).then_inc(s["logits_exp_ready"], 1)

            for t in range(NT + 7):
                if t < NT:
                    act.wait_ge(s["x2nT_full"], t + 1)
                    nc.scalar.activation(xnT[:, t * P:(t + 1) * P], ps[:, 0, 0:P], ACT.Copy).then_inc(s["x2nT_free"], 1)
                if t == TB + 2:
                    root(3)
                if t == HT + 7:
                    root(4)
                k = t - 3
                if 0 <= k < NT:
                    act.wait_ge(s["cross_shifted"], k + 1)
                    if k >= 3:
                        act.wait_ge(s["cross_probsT_full"], k - 2)
                    nc.scalar.activation(cross_p[:, k % 3, :], cross_shift[:, k % 2, :], ACT.Exp).then_inc(s["cross_exp_ready"], 1)
                k = t - 5
                if 0 <= k < NT:
                    act.wait_ge(s["cross_probsT_full"], k + 1)
                    if k >= 2:
                        act.wait_ge(s["cross_out_full"], k - 1)
                    nc.scalar.activation(cross_pT[:, k % 2, 0:4, :], ps[:, 5, :].rearrange("p (c n) -> p c n", c=4), ACT.Copy
                                         ).then_inc(s["cross_probsT_free"], 1)
                    nc.scalar.activation(cross_pT[0:KL, k % 2, 4, :], ps[0:KL, 6, 0:P], ACT.Copy).then_inc(s["cross_probsT_free"], 1)
                if t == HT + 7:
                    logits(0)

            def shared(b):
                for n in range(HC * b, HC * (b + 1)):
                    act.wait_ge(s["shared_relu_ready"], n + 1)
                    if b >= 2:
                        act.wait_ge(s["shared_down_ready"], b - 1)
                    nc.scalar.activation(shared_h[b % 2][:, n % HC, :], shared_relu_buf[:, n % 4, :], ACT.Square).then_inc(s["shared_hidden_ready"], 1)

            root(5)
            for n in range(HC):
                act.wait_ge(s["shared_up_ready"], n + 1)
                nc.scalar.activation(shared_relu_buf[:, n, :], ps[:, 3 + n % 3, :], ACT.Relu).then_inc(s["shared_relu_ready"], 1)
            logits(1)
            shared(0)
            for n in range(2 * ST + 2):
                if n < 2 * ST:
                    act.wait_ge(s["slot_xT_full"], n + 1)
                    if n >= 2:
                        act.wait_ge(s["slot_up_ready"], n - 1)
                    nc.scalar.activation(xslotT[:, n % 2, :], ps[:, n % 2, 0:P], ACT.Copy).then_inc(s["slot_xT_free"], 1)
                k = n - 2
                if k >= 0:
                    act.wait_ge(s["slot_relu_ready"], k + 1)
                    if k >= 2:
                        act.wait_ge(s["slot_down_ready"], k - 1)
                    nc.scalar.activation(hslotT[:, k % 2, :, :], hslot[:, k % 2, :, :], ACT.Square
                                         ).then_inc(s["slot_hidden_ready"], 1)
            for b in range(1, B):
                shared(b)

        @block.vector
        def _(dve):
            chained = [0]

            def chain(ins):
                chained[0] += 1
                ins.then_inc(s["vector_order"], 1)
                dve.wait_ge(s["vector_order"], chained[0])

            def stats_of(lo, hi):
                for t in range(lo, hi):
                    ins = nc.vector.bn_stats(stats[:, t, :], xs[:, t, :])
                    if t == hi - 1:
                        chain(ins)
                aggregate(lo, hi)

            def aggregate(lo, hi):
                for t in range(lo, hi):
                    ins = nc.vector.bn_aggr(mv[:, t, :], stats[:, t, :])
                    if t == hi - 1:
                        chain(ins)

            def variance(k):
                lo, hi = ROOTS[k]
                nc.vector.tensor_scalar_add(rstd[:, lo:hi], mv[:, lo:hi, 1], EPS).then_inc(s["var_ready"], 1)

            def inverse(k, done=None):
                lo, hi = ROOTS[k]
                dve.wait_ge(s["std_ready"], k + 1)
                ins = nc.vector.reciprocal(rstd[:, lo:hi], rstd[:, lo:hi])
                if done:
                    ins.then_inc(s[done], 1)
                else:
                    chain(ins)

            def norm(t):
                return nc.vector.tensor_scalar(xn[:, t, :], xs[:, t, :], mv[:, t, 0:1], rstd[:, t:t + 1],
                                               ALU.subtract, ALU.mult)

            def first_norm(k):
                stats_of(*ROOTS[k])
                variance(k)
                inverse(k)
                for t in range(*ROOTS[k]):
                    norm(t).then_inc(s["xn_ready"], 1)

            dve.wait_ge(s["x0_in"], 16)
            first_norm(0)
            dve.wait_ge(s["wkv_in"], 16)
            for r in (1, 2):
                nc.vector.tensor_copy(w_kv3[:, r * LD:(r + 1) * LD], w_kv3[:, 0:LD]).then_inc(s["latent_w_ready"], 1)
            dve.wait_ge(s["x_in"], 16 * (B - 1))
            first_norm(1)

            def maxes(u, k):
                j, heads = SCORE_TILES[k]
                nn = NS * u + k
                dve.wait_ge(s["scores_ready"], nn + 1)
                if u >= 2 and k == 0:
                    dve.wait_ge(s["max_parts_ready"], u - 1)
                w = (j + 1) * P
                nh = len(heads)
                nc.vector.tensor_reduce(neg_max[:, u % 2, j, heads[0]:heads[0] + nh],
                                        ps[:, score_bank(nn), 0:nh * w].rearrange("p (h n) -> p h n", h=nh), AX.X, ALU.max,
                                        negate=True).then_inc(s["max_ready"], 1)

            def split_max(u):
                dve.wait_ge(s["max_ready"], NS * (u + 1))
                if u >= 2:
                    dve.wait_ge(s["misc_full"], MISC[("m", u - 2)] + 1)
                chain(nc.vector.tensor_copy(max_parts[:, u % 2, :, 0:HG], neg_max[:, u % 2, :, :]))
                nc.vector.tensor_tensor(max_parts[:, u % 2, :, HG:2 * HG], neg_max[:, u % 2, :, :],
                                        max_parts[:, u % 2, :, 0:HG].bitcast(F32), ALU.subtract
                                        ).then_inc(s["max_parts_ready"], 1)

            def misc(use):
                i = MISC[use]
                kind, a = use
                pb = misc_bank(i)
                if kind == "q":
                    b, g = a
                    dve.wait_ge(s["qhi_ready"], G * b + g + 1)
                    nc.vector.tensor_tensor(qlo[:, g, :], pb, qhi[:, g, :].bitcast(F32), ALU.subtract
                                            ).then_inc(s["misc_free"], 1)
                elif kind == "latT":
                    dve.wait_ge(s["latT_hi_ready"], a + 1)
                    nc.vector.tensor_tensor(lstack[LD:2 * LD, a * L:(a + 1) * L], pb[LD:2 * LD, :],
                                            lstack[LD:2 * LD, a * L:(a + 1) * L].bitcast(F32), ALU.subtract
                                            ).then_inc(s["misc_free"], 1)
                elif kind == "lat":
                    dve.wait_ge(s["misc_full"], i + 1)
                    nc.vector.tensor_copy(latent[:, a * TB:(a + 1) * TB, :],
                                          pb[:, 0:TB * LD].rearrange("p (j c) -> p j c", j=TB)
                                          ).then_inc(s["misc_free"], 1)
                elif kind == "den":
                    dve.wait_ge(s["misc_full"], i + 1)
                    nc.vector.reciprocal(rden[:, a % 2, :], pb[:, 0:P]).then_inc(s["misc_free"], 1)
                elif kind == "spread":
                    dve.wait_ge(s["misc_full"], i + 1)
                    b, g = divmod(a, G)
                    if g == 0 and b >= 1:
                        dve.wait_ge(s["misc_full"], MISC[("out", b - 1)] + 1)
                    dve.wait_ge(s["outputs_drained"], a + 1)
                    nc.vector.tensor_tensor(ynT[:, g, :], yraw[:, a % 2, :], pb, ALU.mult
                                            ).then_inc(s["misc_free"], 1)
                elif kind == "out":
                    dve.wait_ge(s["misc_full"], i + 1)
                    nc.vector.tensor_tensor(xs[:, a * TB:(a + 1) * TB, :], pb.rearrange("p (j n) -> p j n", j=TB),
                                            xs[:, a * TB:(a + 1) * TB, :], ALU.add).then_inc(s["misc_free"], 1)

            def add_last(u):
                for pair in range(2):
                    n = ITEMS * u + 6 + pair
                    dve.wait_ge(s["probs_masked"], n + 1)
                    dve.wait_ge(s["sums_added"], 4 * u + 3 + pair)
                    total = prob_sums[:, u % 2, 2 * pair:2 * pair + 2, (TB - 1) * P:L]
                    nc.vector.tensor_tensor(total, total, probT[:, n % PIECES, :, 0:P], ALU.add).then_inc(s["sums_ready"], 1)

            def cx_evacuate(k):
                i = CSETUP[k]
                kind, a = k
                dve.wait_ge(s["csetup_full"], i + 1)
                pb = ps[:, i % 2, :]
                if kind == "kT":
                    ins = nc.vector.tensor_copy(c_kT[:, a, :], pb[:, 0:B * SK])
                elif kind == "vT":
                    ins = nc.vector.tensor_copy(c_vT[:, a, :], pb[:, 0:B * SK])
                elif kind == "G":
                    ins = nc.vector.tensor_scalar(
                        c_G[:, :, a * SK:(a + 1) * SK], pb[:, 0:B * SK].rearrange("p (b s) -> p b s", b=B),
                        float(HD) ** -0.5, None, ALU.mult)
                else:
                    if a >= 4:
                        dve.wait_ge(s[f"values_out{a % 4}"], 16 * (a // 4))
                    ins = nc.vector.tensor_copy(c_V1[:, a % 4, :, :], pb[0:SK, :].rearrange("p (h n) -> p h n", h=4))
                ins.then_inc(s["csetup_free"], 1)

            for use in FIRST_USES:
                misc(use)
            for n in range(NS + LEAD):
                maxes(*divmod(n, NS))
                if n == NS - 1:
                    split_max(0)
            for u in range(NU):
                for t in range(8):
                    for v, k in score_tiles(u, t):
                        maxes(v, k)
                        if k == NS - 1:
                            split_max(v)
                    for k in slot_csetup(u, t):
                        cx_evacuate(k)
                    if t == 0 and u >= 1:
                        add_last(u - 1)
                    for use in slot_misc(u, t):
                        misc(use)
                    b, g = divmod(u, G)
                    if b >= 1 and g == 1 and t == 4:
                        dve.wait_ge(s["misc_free"], MISC[("out", b - 1)] + 1)
                        stats_of((b - 1) * TB, b * TB)
                        if b == B - 1:
                            variance(2)
                    if u == NU - 3 and t == 6:
                        inverse(2, "x2_rstd_ready")
            add_last(NU - 1)
            misc(("den", NU - 1))

            dve.wait_ge(s["consts"], 5)

            def route_stats(hf):
                chain(nc.vector.bn_stats(stats[:, (hf + 1) * HT - 1, :], xs[:, (hf + 1) * HT - 1, :]))
                aggregate(hf * HT, (hf + 1) * HT)
                variance(4 + hf)

            def route_norm(hf):
                inverse(4 + hf)
                for t in range(hf * HT, (hf + 1) * HT):
                    norm(t).then_inc(s["x3n_ready"], 1)

            def route_choice(hf):
                dve.wait_ge(s["logits_exp_ready"], hf + 1)
                prob, oh1, oh2, tmp, tmp2 = (route_tmp[:, i, :, :] for i in range(5))
                chain(nc.vector.tensor_scalar_add(tmp, prob, 1.0))
                chain(nc.vector.reciprocal(prob, tmp))
                for c, oh in enumerate((oh1, oh2)):
                    v, m, first = (prob, tmp2)[c], share[:, hf, c, :], posf[:, c, :]
                    chain(nc.vector.tensor_reduce(m, v, AX.X, ALU.max))
                    chain(nc.vector.tensor_tensor(tmp, v, m.unsqueeze(2).broadcast_to([P, HT, E]), ALU.is_equal))
                    chain(nc.vector.tensor_tensor(tmp, tmp, first_of[:, :].unsqueeze(1).broadcast_to([P, HT, E]), ALU.mult))
                    chain(nc.vector.tensor_reduce(first, tmp, AX.X, ALU.max))
                    chain(nc.vector.tensor_tensor(oh, tmp, first.unsqueeze(2).broadcast_to([P, HT, E]), ALU.is_equal))
                    if c == 0:
                        chain(nc.vector.scalar_tensor_tensor(tmp2, oh, -4.0, prob, ALU.mult, ALU.add))
                nc.vector.tensor_tensor(chosen[:, :, :], oh1, oh2, ALU.add).then_inc(s["choice_ready"], 1)
                dve.wait_ge(s["choice_ready"], hf + 1)

            def route_shares(hf):
                chain(nc.vector.tensor_tensor(posf[:, 0, :], share[:, hf, 0, :], share[:, hf, 1, :], ALU.add))
                chain(nc.vector.tensor_scalar_add(posf[:, 0, :], posf[:, 0, :], 1e-6))
                chain(nc.vector.reciprocal(posf[:, 1, :], posf[:, 0, :]))
                for c in range(2):
                    chain(nc.vector.tensor_tensor(share[:, hf, c, :], share[:, hf, c, :], posf[:, 1, :], ALU.mult))

            def route_slots(hf):
                oh1, oh2, tmp, tmp2 = (route_tmp[:, i, :, :] for i in range(1, 5))
                dve.wait_ge(s["counts_ready"], hf + 1)
                pre = ps[:, LOGIT_BANK[hf], hf * P:hf * P + HT * E]
                cnt = ps[:, LOGIT_BANK[hf], hf * P + HT * E:hf * P + (HT + 1) * E]
                tiles, first, through = (tstat[:, i, :] for i in range(3))
                chain(nc.vector.tensor_tensor(pairs_tmp[:, :, 0:HT], cnt.unsqueeze(2).broadcast_to([P, E, HT]), tile_bounds[:, :, :],
                                              ALU.is_gt))
                chain(nc.vector.tensor_reduce(tiles, pairs_tmp[:, :, 0:HT], AX.X, ALU.add))
                chain(nc.vector.tensor_tensor(pairs_tmp[:, :, :], tiles.unsqueeze(1).broadcast_to([P, E, E]), lower[:, :, :],
                                              ALU.mult))
                chain(nc.vector.tensor_reduce(first, pairs_tmp[:, :, :], AX.X, ALU.add))
                chain(nc.vector.tensor_tensor(through, first, tiles, ALU.add))
                chain(nc.vector.tensor_scalar(first, first, float(P), None, ALU.mult))
                chain(nc.vector.tensor_tensor(tmp2, pre.rearrange("p (t e) -> p t e", e=E),
                                              first.unsqueeze(1).broadcast_to([P, HT, E]), ALU.add))
                for c, oh in enumerate((oh1, oh2)):
                    chain(nc.vector.tensor_tensor(tmp, tmp2, oh, ALU.mult))
                    chain(nc.vector.tensor_reduce(posf[:, c, :], tmp, AX.X, ALU.add))
                chain(nc.vector.tensor_copy(posi[:, hf, :, :], posf[:, :, :]))
                chain(nc.vector.tensor_tensor(tile_past[:, :, :], through.unsqueeze(1).broadcast_to([P, ST, E]),
                                              tile_index[:, :].unsqueeze(2).broadcast_to([P, ST, E]), ALU.is_le))
                chain(nc.vector.tensor_reduce(tile_expert_f[:, hf, :], tile_past[:, :, :], AX.X, ALU.add))
                chain(nc.vector.tensor_scalar(tile_expert_f[:, hf, :], tile_expert_f[:, hf, :], float(E - 1), None, ALU.min))
                nc.vector.tensor_copy(tile_expert[:, hf, :], tile_expert_f[:, hf, :]).then_inc(s["slots_ready"], 1)
                dve.wait_ge(s["slots_ready"], hf + 1)

            for t in range(NT + 7):
                k = t - 7
                if k >= 0:
                    dve.wait_ge(s["residual_biased"], k + 1)
                    dve.wait_ge(s["cross_out_full"], k + 1)
                    nc.vector.tensor_tensor(xs[:, k, :], ps[:, 7, 0:P], xs[:, k, :], ALU.add
                                            ).then_inc(s["cross_out_free"], 1)
                    if k % HT:
                        dve.wait_ge(s["cross_out_free"], k)
                        nc.vector.bn_stats(stats[:, k - 1, :], xs[:, k - 1, :])
                if t == HT + 8:
                    route_choice(0)
                k = t - 2
                if 0 <= k < NT:
                    dve.wait_ge(s["cross_scores_ready"], k + 1)
                    sc = ps[:, 1 + 2 * (k % 2):3 + 2 * (k % 2), 0:KV // 2].rearrange("p a (h s) -> p a h s", s=SK)
                    mx = cstat[:, k % 2, 0, :].rearrange("p (a h) -> p a h", a=2)
                    chain(nc.vector.tensor_reduce(mx, sc, AX.X, ALU.max))
                    if k == 0:
                        dve.wait_ge(s["outputs_ready"], TB * NU)
                        dve.wait_ge(s["sums_begun"], 2 * NU)
                        dve.wait_ge(s["probs_masked"], ITEMS * NU)
                    if k >= 2:
                        dve.wait_ge(s["cross_exp_ready"], k - 1)
                    nc.vector.tensor_tensor(
                        cross_shift[:, k % 2, :].rearrange("p (a h s) -> p a h s", a=2, s=SK), sc,
                        mx.unsqueeze(3).broadcast_to([P, 2, CH // 2, SK]), ALU.subtract).then_inc(s["cross_shifted"], 1)
                if t == 1:
                    misc(("spread", NU - 1))
                if t == 3:
                    misc(("out", B - 1))
                if t == TB + 1:
                    dve.wait_ge(s["misc_free"], len(order))
                    stats_of(NT - TB, NT)
                    variance(3)
                if t == TB + 3:
                    inverse(3, "x2_rstd_ready")
                if t == HT + 7:
                    route_norm(0)
                k = t - 3
                if 0 <= k < NT:
                    dve.wait_ge(s["cross_exp_ready"], k + 1)
                    chain(nc.vector.tensor_reduce(cstat[:, k % 2, 1, :],
                                                  cross_p[:, k % 3, :].rearrange("p (h s) -> p h s", s=SK), AX.X, ALU.add))
                    if k >= 2:
                        dve.wait_ge(s["cross_probs_ready"], k - 1)
                    nc.vector.reciprocal(cstat[:, k % 2, 2, :], cstat[:, k % 2, 1, :]).then_inc(s["cross_rsum_ready"], 1)
                if t == HT + 6:
                    dve.wait_ge(s["cross_out_free"], HT)
                    route_stats(0)
                if t == HT + 9:
                    route_slots(0)
                if t == HT + 10:
                    route_shares(0)
            dve.wait_ge(s["cross_out_free"], NT)
            route_stats(1)
            route_norm(1)
            route_choice(1)
            route_slots(1)
            route_shares(1)
            dve.wait_ge(s["ffn_w_in"], 32)

            def shared(b):
                for n in range(HC * b, HC * (b + 1)):
                    dve.wait_ge(s["shared_up_ready"], n + 1)
                    if n >= 4:
                        dve.wait_ge(s["shared_hidden_ready"], n - 3)
                    nc.vector.tensor_scalar(shared_relu_buf[:, n % 4, :], ps[:, 3 + n % 3, :], 0.0, None, ALU.max
                                            ).then_inc(s["shared_relu_ready"], 1)

            def shared_add(b):
                dve.wait_ge(s["shared_down_ready"], b + 1)
                nc.vector.tensor_tensor(acc[:, b * TB:(b + 1) * TB, :], ps[:, 6 + b % 2, :].rearrange(
                    "p (j n) -> p j n", j=TB), acc[:, b * TB:(b + 1) * TB, :], ALU.add).then_inc(s["shared_added"], 1)

            def combine(t):
                hf, j = divmod(t, HT)
                dve.wait_ge(s[f"gathered{t}"], 32)
                chain(nc.vector.scalar_tensor_tensor(acc[:, t, :], gathered_y[:, hf, j, 0, :], share[:, hf, 0, j:j + 1],
                                                     acc[:, t, :], ALU.mult, ALU.add))
                nc.vector.scalar_tensor_tensor(acc[:, t, :], gathered_y[:, hf, j, 1, :], share[:, hf, 1, j:j + 1],
                                               acc[:, t, :], ALU.mult, ALU.add).then_inc(s["combined"], 1)

            shared_add(0)
            for n in range(2 * ST + 3):
                if n < 2 * ST:
                    if n >= 2:
                        dve.wait_ge(s["slot_up_ready"], n - 1)
                    e = nc.vector.value_load(tile_expert[0:1, n // ST, n % ST:n % ST + 1], min_val=0, max_val=E - 1)
                    nc.vector.tensor_copy(f_upE[:, n % 2, :], f_up[:, bass.ds(e, 1), :].rearrange("p a n -> p (a n)")
                                          ).then_inc(s["slot_weights_ready"], 1)
                k = n - 1
                if 0 <= k < 2 * ST:
                    dve.wait_ge(s["slot_up_ready"], k + 1)
                    if k >= 2:
                        dve.wait_ge(s["slot_hidden_ready"], k - 1)
                    nc.vector.tensor_scalar(hslot[:, k % 2, :, :], ps[:, 2 + k % 2, :].rearrange(
                        "p (c n) -> p c n", c=HC), 0.0, None, ALU.max).then_inc(s["slot_relu_ready"], 1)
                k = n - 3
                if k >= 0:
                    dve.wait_ge(s["slot_down_ready"], k + 1)
                    if k >= 4:
                        dve.wait_ge(s[f"slot_y_out{k % 4}"], 16 * (k // 4))
                    nc.vector.tensor_copy(ystage[:, k % 4, :], ps[:, 6 + k % 2, 0:D]).then_inc(s["slot_y_ready"], 1)
                    if k >= 2 * ST - HT - 1 and k - (2 * ST - HT - 1) < HT:
                        combine(k - (2 * ST - HT - 1))
            dve.wait_ge(s["combined"], HT)
            for b in range(1, B):
                shared(b)
                if b == 2:
                    shared_add(1)
            dve.wait_ge(s["shared_added"], 2)
            for b in range(2, B):
                ready = (b + 1) * TB - (b == B - 1)
                for t in range(b * TB, ready):
                    combine(t)
                dve.wait_ge(s["combined"], ready)
                shared_add(b)
            dve.wait_ge(s["shared_added"], B)
            combine(NT - 1)

        @block.tensor
        def _(pe):
            def build(k):
                i = SETUP[k]
                kind, a = k
                if i >= SETUP_BANKS:
                    pe.wait_ge(s["setup_free"], i - SETUP_BANKS + 1)
                bank = i % SETUP_BANKS
                if kind == "xT":
                    pe.wait_ge(s["consts"], 1)
                    pe.wait_ge(s["xn_ready"], TB * (a + 1))
                    for j in range(TB):
                        last = nc.tensor.transpose(ps[:, bank, j * P:(j + 1) * P], xn[:, a * TB + j, :], ident[:, :])
                elif kind == "A":
                    pe.wait_ge(s["wA_in"], 32)
                    r = a * HD
                    for i in range(H // 2):
                        last = nc.tensor.matmul(ps[:, bank, i * LD:(i + 1) * LD], w_qT[r:r + HD, i, :],
                                                w_kT[r:r + HD, i, :], start=True, stop=True)
                else:
                    pe.wait_ge(s["wB_in"], 32)
                    r = a * HD
                    for h in range(a, H, 2):
                        q = (h % HG) * LD
                        last = nc.tensor.matmul(ps[q:q + LD, bank, (h // HG) * D:(h // HG + 1) * D],
                                                w_vT[r:r + HD, h // 2, :], w_out[r:r + HD, h // 2, :],
                                                start=True, stop=True)
                last.then_inc(s["setup_full"], 1)

            def cx_build(k):
                i = CSETUP[k]
                kind, a = k
                if i == 0:
                    pe.wait_ge(s["max_ready"], NS * NU)
                    pe.wait_ge(s["cross_w_in"], 96)
                if i >= 2:
                    pe.wait_ge(s["csetup_free"], i - 1)
                bank = i % 2
                if kind in ("kT", "vT"):
                    w = c_k if kind == "kT" else c_v
                    last = nc.tensor.matmul(ps[:, bank, 0:B * SK], w[:, a * P:(a + 1) * P], c_T[:, :],
                                            start=True, stop=True)
                elif kind == "G":
                    r = (a % 2) * HD
                    last = nc.tensor.matmul(ps[:, bank, 0:B * SK], c_qT[r:r + HD, a // 2, :], c_kT[r:r + HD, a // 2, :],
                                            start=True, stop=True)
                else:
                    if a == 0:
                        pe.wait_ge(s["csetup_free"], CSETUP[("vT", CH // 2 - 1)] + 1)
                    b, half = divmod(a, 2)
                    r = half * HD
                    for hh in range(4):
                        h = 2 * hh + half
                        last = nc.tensor.matmul(ps[0:SK, bank, hh * D:(hh + 1) * D],
                                                c_vT[r:r + HD, h // 2, b * SK:(b + 1) * SK],
                                                c_o[r:r + HD, h // 2, :], start=True, stop=True)
                last.then_inc(s["csetup_full"], 1)

            for k in setup[:setup1]:
                build(k)
            pe.wait_ge(s["setup_free"], setup1)
            pe.wait_ge(s["latent_w_ready"], 2)

            def misc(use):
                i = MISC[use]
                kind, a = use
                if i >= 2 or i == len(FIRST_USES):
                    pe.wait_ge(s["misc_free"], i - 1 if i < len(FIRST_USES) else i)
                pb = misc_bank(i)
                if kind == "latT":
                    last = nc.tensor.matmul(pb[0:R3, :], w_kv3[:, :], xnT[:, a * L:(a + 1) * L], start=True, stop=True)
                elif kind == "lat":
                    for j in range(TB):
                        t = a * TB + j
                        last = nc.tensor.matmul(pb[:, j * LD:(j + 1) * LD], xnT[:, t * P:(t + 1) * P], w_kv3[:, 0:LD],
                                                start=True, stop=True)
                elif kind == "q":
                    b, g = a
                    last = nc.tensor.matmul(pb, wA[:, g * P:(g + 1) * P], xnT[:, b * L:(b + 1) * L], start=True,
                                            stop=True)
                elif kind == "m":
                    pe.wait_ge(s["max_parts_ready"], a + 1)
                    for j in range(TB):
                        last = nc.tensor.transpose(pb[0:2 * HG, j * P:(j + 1) * P],
                                                   max_parts[:, a % 2, j, :].bitcast(F32), ident[:, :])
                elif kind == "den":
                    pe.wait_ge(s["sums_begun"], 2 * (a + 1))
                    pe.wait_ge(s["sums_ready"], 2 * (a + 1))
                    for j in range(TB):
                        for h in range(HG):
                            last = nc.tensor.matmul(ps[h * LD:(h + 1) * LD, MISC_BANK, 0:P], to_rows[:, j, :],
                                                    prob_sums[:, a % 2, h, j * P:(j + 1) * P], start=j == 0, stop=j == TB - 1)
                elif kind == "spread":
                    pe.wait_ge(s["misc_free"], MISC[("den", a)] + 1)
                    for j in range(TB):
                        last = nc.tensor.matmul(pb[:, j * P:(j + 1) * P], from_rows[:, j, :], rden[:, a % 2, :],
                                                start=True, stop=True)
                else:
                    for j in range(TB):
                        for g in range(G):
                            last = nc.tensor.matmul(pb[:, j * D:(j + 1) * D], ynT[:, g, j * P:(j + 1) * P], wB[:, g, :],
                                                    start=g == 0, stop=g == G - 1)
                last.then_inc(s["misc_full"], 1)

            def scores(u, k):
                b, g = divmod(u, G)
                j, heads = SCORE_TILES[k]
                nn = NS * u + k
                if u == 0 and k == 0:
                    pe.wait_ge(s["qstack_first"], 16 * 3 * HG)
                    pe.wait_ge(s["misc_free"], MISC[("latT", b)] + 1)
                if k == 0 and u == 1 or k == 0 and g == 0 and b >= 1:
                    pe.wait_ge(s[f"qstack{b % 2}"], 16 * 3 * HG * (b // 2 + 1))
                    pe.wait_ge(s["misc_free"], MISC[("latT", b)] + 1)
                if nn == NS + LEAD:
                    pe.wait_ge(s["max_ready"], nn)
                elif nn > NS + LEAD:
                    pe.wait_ge(s["max_ready"], nn - 1)
                elif nn >= 6:
                    pe.wait_ge(s["max_ready"], nn - 5)
                w = (j + 1) * P
                for m, hh in enumerate(heads):
                    h = g * HG + hh
                    nc.tensor.matmul(ps[:, score_bank(nn), m * w:(m + 1) * w], qstack[b % 2][0:R3, h, j * P:(j + 1) * P],
                                     lstack[0:R3, b * L:b * L + w], start=True, stop=False)
                    last = nc.tensor.matmul(ps[:, score_bank(nn), (m + 1) * w - P:(m + 1) * w], identb[:, :], mask_qk[:, :],
                                            start=False, stop=True)
                last.then_inc(s["scores_ready"], 1)

            def scoresT(n):
                u, t = divmod(n, ITEMS)
                b, g = divmod(u, G)
                i, pair = divmod(t, 2)
                w = L - i * P
                if n == 0:
                    pe.wait_ge(s["max_ready"], NS + LEAD)
                if t == 0:
                    pe.wait_ge(s[f"max_rows{u % 2}"], 32 * (u // 2 + 1))
                if n >= 2:
                    pe.wait_ge(s["probs_ready"], n - 1)
                for k in range(2):
                    h = g * HG + pair * 2 + k
                    bank = 2 + 2 * (n % 2) + k
                    last = nc.tensor.matmul(ps[:, bank, 0:w], lstack[:, b * L + i * P:b * L + (i + 1) * P],
                                            qstack[b % 2][:, h, i * P:L], start=True, stop=True)
                last.then_inc(s["scoresT_ready"], 1)

            def pv(n):
                u, i = divmod(n, TB)
                b, g = divmod(u, G)
                w = L - i * P
                pe.wait_ge(s["probs_masked"], 2 * n + 2)
                if i == 0 and g == 0:
                    pe.wait_ge(s["misc_free"], MISC[("lat", b)] + 1)
                if i == 0 and u >= 1:
                    pe.wait_ge(s["outputs_drained"], u)
                for h in range(HG):
                    last = nc.tensor.matmul(ps[h * LD:(h + 1) * LD, OUT_BANK, i * P:L], latent[:, b * TB + i, :],
                                            probT[:, (2 * n + h // 2) % PIECES, h % 2, 0:w], start=i == 0, stop=i == TB - 1)
                last.then_inc(s["outputs_ready"], 1)

            for use in FIRST_USES:
                misc(use)
            for k in setup[setup1:]:
                build(k)
            pe.wait_ge(s["setup_free"], len(setup))
            pe.wait_ge(s["consts"], 4)
            for n in range(NS + LEAD):
                scores(*divmod(n, NS))
                if n == NS + 1:
                    misc(("m", 0))
            for u in range(NU):
                for t in range(8):
                    n = ITEMS * u + t
                    scoresT(n)
                    for v, k in score_tiles(u, t):
                        scores(v, k)
                    for k in slot_csetup(u, t):
                        cx_build(k)
                    if t % 2 == 0 and n >= 4:
                        pv(n // 2 - 2)
                    for use in slot_misc(u, t):
                        misc(use)
            pv(TB * NU - 2)
            pv(TB * NU - 1)
            misc(("den", NU - 1))

            def logits(hf):
                for b in (2 * hf, 2 * hf + 1):
                    pe.wait_ge(s["x3n_ready"], TB * (b + 1))
                    if hf == 0 and b == 0:
                        pe.wait_ge(s["x2nT_free"], HT + 8)
                    if b == 1:
                        pe.wait_ge(s["x3nT_free"], b)
                    for j in range(TB):
                        last = nc.tensor.transpose(ps[:, TRANSPOSE_BANK[b], j * P:(j + 1) * P], xn[:, b * TB + j, :], ident[:, :])
                    last.then_inc(s["x3nT_full"], 1)
                pe.wait_ge(s["x3nT_free"], 2 * hf + 2)
                pe.wait_ge(s["router_w_in"], 16)
                pe.wait_ge(s["consts"], 5)
                for j in range(HT):
                    t = hf * HT + j
                    last = nc.tensor.matmul(ps[:, LOGIT_BANK[hf], hf * P + j * E:hf * P + (j + 1) * E],
                                            xnT[:, t * P:(t + 1) * P], w_r[:, :], start=True, stop=True)
                last.then_inc(s["logits_ready"], 1)

            def counts(hf):
                at = hf * P
                pe.wait_ge(s["choice_ready"], hf + 1)
                for j in range(HT):
                    for i in range(j + 1):
                        nc.tensor.matmul(ps[:, LOGIT_BANK[hf], at + j * E:at + (j + 1) * E],
                                         below[:, :] if i == j else ones[:, :], chosen[:, i, :], start=i == 0, stop=i == j)
                for i in range(HT):
                    last = nc.tensor.matmul(ps[:, LOGIT_BANK[hf], at + HT * E:at + (HT + 1) * E], ones[:, :], chosen[:, i, :],
                                            start=i == 0, stop=i == HT - 1)
                last.then_inc(s["counts_ready"], 1)

            for t in range(NT + 7):
                if t == HT + 9:
                    counts(0)
                if t < NT:
                    pe.wait_ge(s["x2n_ready"], t + 1)
                    if t >= 1:
                        pe.wait_ge(s["x2nT_free"], t)
                    if t == HT + 8:
                        pe.wait_ge(s["logits_exp_ready"], 1)
                    nc.tensor.transpose(ps[:, 0, 0:P], xn[:, t, :], ident[:, :]).then_inc(s["x2nT_full"], 1)
                if t == 1:
                    misc(("spread", NU - 1))
                if t == 2:
                    misc(("out", B - 1))
                    pe.wait_ge(s["probs_ready"], ITEMS * NU)
                    pe.wait_ge(s["csetup_free"], len(csetup))
                if t == TB:
                    pe.wait_ge(s["misc_free"], len(order))
                    pe.wait_ge(s["values_back"], 32 * B)
                k = t - 2
                if 0 <= k < NT:
                    pe.wait_ge(s["x2nT_free"], k + 1)
                    if k >= 2:
                        pe.wait_ge(s["cross_shifted"], k - 1)
                    for half in range(2):
                        last = nc.tensor.matmul(ps[:, 1 + 2 * (k % 2) + half, 0:KV // 2], xnT[:, k * P:(k + 1) * P],
                                                c_G[:, k // TB, half * (KV // 2):(half + 1) * (KV // 2)],
                                                start=True, stop=True)
                    last.then_inc(s["cross_scores_ready"], 1)
                k = t - 5
                if 0 <= k < NT:
                    pe.wait_ge(s["cross_probs_ready"], k + 1)
                    if k >= 1:
                        pe.wait_ge(s["cross_probsT_free"], 2 * k)
                    for c in range(KC):
                        w = P if c < KC - 1 else KL
                        last = nc.tensor.transpose(ps[0:w, 5 + c // 4, (c % 4) * P:(c % 4 + 1) * P],
                                                   cross_p[:, k % 3, c * P:c * P + w], ident[:, :])
                    last.then_inc(s["cross_probsT_full"], 1)
                k = t - 6
                if 0 <= k < NT:
                    pe.wait_ge(s["cross_probsT_free"], 2 * k + 2)
                    if k >= 1:
                        pe.wait_ge(s["cross_out_free"], k)
                    for c in range(KC):
                        w = P if c < KC - 1 else KL
                        last = nc.tensor.matmul(ps[:, 7, 0:P], cross_pT[0:w, k % 2, c, :], c_V[0:w, k // TB, c, :],
                                                start=c == 0, stop=c == KC - 1)
                    last.then_inc(s["cross_out_full"], 1)
                if t == HT + 7:
                    logits(0)
            pe.wait_ge(s["ffn_w_in"], 32)
            pe.wait_ge(s["cross_out_free"], NT)
            pe.wait_ge(s["slots_ready"], 1)

            def shared_up(b):
                for n in range(HC * b, HC * (b + 1)):
                    if n >= 3:
                        pe.wait_ge(s["shared_relu_ready"], n - 2)
                    nc.tensor.matmul(ps[:, 3 + n % 3, :], f_up[:, NE - 1, (n % HC) * P:(n % HC + 1) * P],
                                     xnT[:, b * L:(b + 1) * L], start=True, stop=True).then_inc(s["shared_up_ready"], 1)

            def shared_down(b):
                pe.wait_ge(s["shared_hidden_ready"], HC * (b + 1))
                for j in range(TB):
                    for c in range(HC):
                        last = nc.tensor.matmul(ps[:, 6 + b % 2, j * P:(j + 1) * P], shared_h[b % 2][:, c, j * P:(j + 1) * P],
                                                f_dn[:, NE - 1, c, :], start=c == 0, stop=c == HC - 1)
                last.then_inc(s["shared_down_ready"], 1)

            shared_up(0)
            logits(1)
            counts(1)
            shared_down(0)
            experts = {}
            for n in range(2 * ST + 3):
                if n == 3:
                    pe.wait_ge(s["shared_added"], 1)
                    pe.wait_ge(s["slots_ready"], 2)
                if n < 2 * ST:
                    hf, t = divmod(n, ST)
                    experts[n] = nc.tensor.value_load(tile_expert[0:1, hf, t:t + 1], min_val=0, max_val=E - 1)
                    pe.wait_ge(s[f"slot_x_in{n % 4}"], 16 * (n // 4 + 1))
                    if n >= 2:
                        pe.wait_ge(s["slot_xT_free"], n - 1)
                    nc.tensor.transpose(ps[:, n % 2, 0:P], xg[:, n % 4, :], ident[:, :]).then_inc(s["slot_xT_full"], 1)
                k = n - 1
                if 0 <= k < 2 * ST:
                    hf, t = divmod(k, ST)
                    pe.wait_ge(s["slot_xT_free"], k + 1)
                    if k >= 2:
                        pe.wait_ge(s["slot_relu_ready"], k - 1)
                    pe.wait_ge(s["slot_weights_ready"], k + 1)
                    for c in range(HC):
                        last = nc.tensor.matmul(ps[:, 2 + k % 2, c * P:(c + 1) * P], f_upE[:, k % 2, c * P:(c + 1) * P],
                                                xslotT[:, k % 2, :], start=True, stop=True)
                    last.then_inc(s["slot_up_ready"], 1)
                k = n - 3
                if k >= 0:
                    hf, t = divmod(k, ST)
                    pe.wait_ge(s["slot_hidden_ready"], k + 1)
                    if k >= 2:
                        pe.wait_ge(s["slot_y_ready"], k - 1)
                    e = experts[k]
                    for c in range(HC):
                        last = nc.tensor.matmul(ps[:, 6 + k % 2, 0:D], hslotT[:, k % 2, c, :],
                                                f_dn[:, bass.ds(e, 1), c, :].rearrange("p a n -> p (a n)"),
                                                start=c == 0, stop=c == HC - 1)
                    last.then_inc(s["slot_down_ready"], 1)
            pe.wait_ge(s["slot_relu_ready"], 2 * ST)
            for b in range(1, B):
                shared_up(b)
                if b == 2:
                    pe.wait_ge(s["slot_y_ready"], 2 * ST)
                if b >= 2:
                    shared_down(b - 1)
            shared_down(B - 1)


def kernel(x, ctx_768, L0_attn_Wq, L0_attn_Wkv_down, L0_attn_Wk_up, L0_attn_Wv_up, L0_attn_Wout, L0_xattn_Wq,
           L0_xattn_Wk, L0_xattn_Wv, L0_xattn_Wo, L0_xattn_bo, L0_ffn_W_router, L0_ffn_W_up, L0_ffn_W_down,
           L0_ffn_W_sh_up, L0_ffn_W_sh_down):
    import numpy as np
    import concourse.bacc as bacc
    from concourse.bass_utils import run_bass_kernel_spmd

    def pairs(a):
        h, k, n = a.shape
        return a.reshape(h // 2, 2, k, n).transpose(1, 2, 0, 3).reshape(2 * k, h // 2, n)

    a = {k: np.asarray(v) for k, v in locals().items() if k.startswith("L0") or k in ("x", "ctx_768")}
    ch = a["L0_xattn_Wq"].shape[1] // 64
    d = a["x"].shape[2]
    up = np.concatenate([a["L0_ffn_W_up"], a["L0_ffn_W_sh_up"][None]])
    dn = np.concatenate([a["L0_ffn_W_down"], a["L0_ffn_W_sh_down"][None]])
    ins = {
        "x": a["x"],
        "ctxT": a["ctx_768"].transpose(2, 0, 1),
        "wqT": pairs(a["L0_attn_Wq"].transpose(1, 2, 0)),
        "wkT": pairs(a["L0_attn_Wk_up"].transpose(1, 2, 0)),
        "wvT": pairs(a["L0_attn_Wv_up"].transpose(1, 2, 0)),
        "wout": pairs(a["L0_attn_Wout"]),
        "wkv": a["L0_attn_Wkv_down"],
        "cwqT": pairs(a["L0_xattn_Wq"].T.reshape(ch, 64, d)),
        "cwk": a["L0_xattn_Wk"],
        "cwv": a["L0_xattn_Wv"],
        "cwo": pairs(a["L0_xattn_Wo"].reshape(ch, 64, d)),
        "cbo": np.broadcast_to(a["L0_xattn_bo"], (128, d)),
        "wr": a["L0_ffn_W_router"],
        "wup": up.transpose(1, 0, 2),
        "wdown": dn.reshape(dn.shape[0], -1, 128, d).transpose(2, 0, 1, 3),
    }
    nc = bacc.Bacc("TRN2", target_bir_lowering=False, num_devices=1)
    arrays = {f"in_{k}": np.ascontiguousarray(v) for k, v in ins.items()}
    aps = [nc.dram_tensor(k, v.shape, mybir.dt.from_np(v.dtype), kind="ExternalInput").ap() for k, v in arrays.items()]
    b, sk = a["ctx_768"].shape[:2]
    vscr = nc.dram_tensor("value_scratch", (b, ch, sk, d), F32, kind="Internal").ap()
    ns = slot_tiles(x.shape[0] * x.shape[1] // 2, a["L0_ffn_W_router"].shape[1]) * 128
    xslot = [nc.dram_tensor(f"x_slots{i}", (ns, d), F32, kind="Internal").ap() for i in range(2)]
    yslot = [nc.dram_tensor(f"y_slots{i}", (ns, d), F32, kind="Internal").ap() for i in range(2)]
    out = nc.dram_tensor("out_x", a["x"].shape, F32, kind="ExternalOutput").ap()
    decoder_layer(nc, *aps, vscr, xslot, yslot, out)
    r = run_bass_kernel_spmd(nc, [arrays], core_ids=[0])
    return r.results[0]["out_x"]
```
